# Optimizing a Trainium2 kernel written in Bass

```python
import numpy as np
import jax
import jax.numpy as jnp

def _softmax(x, axis=-1):
    return jax.nn.softmax(x, axis=axis)

def _gelu(x):
    return jax.nn.gelu(x, approximate=True)

def _silu(x):
    return jax.nn.silu(x)

def _sigmoid(x):
    return jax.nn.sigmoid(x)

def _layernorm(x, axis=-1, eps=1e-05):
    m = jnp.mean(x, axis=axis, keepdims=True)
    v = jnp.var(x, axis=axis, keepdims=True)
    return (x - m) / jnp.sqrt(v + eps)

def _scatter_add(tgt, idx, src, axis=0):
    return tgt.at[idx].add(src)

def _segment_sum(src, seg, n):
    return jax.ops.segment_sum(src, seg, n)
kernel_name = 'mk_cond_resid_d4_seqx_r4_90a2d9'

def setup_inputs(seed: int=0):
    np.random.seed(seed)
    _w = jnp.asarray

    def _rec_inputs():
        import jax
        import jax.numpy as jnp
        _rk = jax.random.key(seed)
        x = -0.0002071 + 1 * jax.random.normal(jax.random.fold_in(_rk, 1), (64, 64, 256), jnp.float32)
        _lenS = 64 - jax.random.randint(jax.random.fold_in(_rk, 7), (64,), 0, max(1, 64 // 4) + 1, jnp.int32)
        _lenS2 = 64 - jax.random.randint(jax.random.fold_in(_rk, 8), (64,), 0, max(1, 64 // 4) + 1, jnp.int32)
        cond_8 = jax.random.uniform(jax.random.fold_in(_rk, 11), (64, 8), jnp.float32, 0.0, 0.983423)
        return (x, cond_8)
    x, cond_8 = _rec_inputs()

    def _L0_cond_setup():
        import jax, jax.numpy as jnp
        import numpy as np
        R = 16
        ALPHA = 32.0
        SCALING = ALPHA / R
        key = jax.random.key(seed)
        ks = jax.random.split(key, 6)
        B, T, C, O, E = (16, 375, 256, 256, 8)
        x = jax.random.normal(ks[0], (B, T, C), dtype=jnp.float32)
        w = jax.random.uniform(ks[1], (B, E), dtype=jnp.float32)
        W_base = jax.random.normal(ks[2], (O, C), dtype=jnp.float32) * 0.02
        b_base = jax.random.normal(ks[3], (O,), dtype=jnp.float32) * 0.02
        As = jax.random.normal(ks[4], (E, R, C), dtype=jnp.float32) * 0.02
        Bs = jax.random.normal(ks[5], (E, O, R), dtype=jnp.float32) * 0.02
        return {'x': x, 'w': w, 'W_base': W_base, 'b_base': b_base, 'As': As, 'Bs': Bs}
    _L0_cond_all = _L0_cond_setup()
    _L0_cond_in = {k: v for k, v in _L0_cond_all.items() if k in ('W_base', 'b_base', 'As', 'Bs')}
    del _L0_cond_all

    def _L1_cond_setup():
        import jax, jax.numpy as jnp
        import numpy as np
        TOP_K = 2
        NUM_MOE_LAYERS = 12

        def _gemma_mlp(x, gate_w, up_w, down_w):
            g = jnp.einsum('bsh,hi->bsi', x, gate_w)
            u = jnp.einsum('bsh,hi->bsi', x, up_w)
            return jnp.einsum('bsi,ih->bsh', jax.nn.gelu(g, approximate=True) * u, down_w)
        key = jax.random.key(seed)
        ks = jax.random.split(key, 8)
        B, S, H, I, E = (32, 64, 256, 1024, 8)
        std = 0.02
        return {'x': jax.random.normal(ks[0], (B, S, H), jnp.float32), 'router_logits': jax.random.normal(ks[1], (B, E), jnp.float32), 'skill_gate': jax.random.normal(ks[2], (E, H, I), jnp.float32) * std, 'skill_up': jax.random.normal(ks[3], (E, H, I), jnp.float32) * std, 'skill_down': jax.random.normal(ks[4], (E, I, H), jnp.float32) * std, 'shared_gate': jax.random.normal(ks[5], (H, I), jnp.float32) * std, 'shared_up': jax.random.normal(ks[6], (H, I), jnp.float32) * std, 'shared_down': jax.random.normal(ks[7], (I, H), jnp.float32) * std}
    _L1_cond_all = _L1_cond_setup()
    _L1_cond_in = {k: v for k, v in _L1_cond_all.items() if k in ('skill_gate', 'skill_up', 'skill_down', 'shared_gate', 'shared_up', 'shared_down')}
    del _L1_cond_all

    def _L2_cond_setup():
        import jax, jax.numpy as jnp
        import numpy as np
        B, S, D = (16, 512, 256)
        E, H = (8, 512)
        key = jax.random.key(seed)
        ks = jax.random.split(key, 8)
        scale = 0.02
        x = jax.random.normal(ks[0], (B, S, D), dtype=jnp.float32)
        opcode_onehot = jax.random.uniform(ks[1], (B, E), dtype=jnp.float32)
        W_up = jax.random.normal(ks[2], (E, H, D), dtype=jnp.float32) * scale
        b_up = jnp.zeros((E, H), dtype=jnp.float32)
        W_gate = jax.random.normal(ks[3], (E, H, D), dtype=jnp.float32) * scale
        b_gate = jnp.zeros((E, H), dtype=jnp.float32)
        W_down = jax.random.normal(ks[4], (E, D, H), dtype=jnp.float32) * scale
        b_down = jnp.zeros((E, D), dtype=jnp.float32)
        return {'x': x, 'opcode_onehot': opcode_onehot, 'W_up': W_up, 'b_up': b_up, 'W_gate': W_gate, 'b_gate': b_gate, 'W_down': W_down, 'b_down': b_down}
    _L2_cond_all = _L2_cond_setup()
    _L2_cond_in = {k: v for k, v in _L2_cond_all.items() if k in ('W_up', 'b_up', 'W_gate', 'b_gate', 'W_down', 'b_down')}
    del _L2_cond_all

    def _L3_cond_setup():
        import jax, jax.numpy as jnp
        import numpy as np
        key = jax.random.key(seed)
        k1, k2, k3, k4, k5 = jax.random.split(key, 5)
        B, N, T, O, G = (32, 64, 256, 256, 8)
        x = jax.random.normal(k1, (B, N, T), dtype=jnp.float32)
        y = jax.random.uniform(k2, (B, G), dtype=jnp.float32)
        weight = jax.random.normal(k3, (G, O, T), dtype=jnp.float32) * (1.0 / np.sqrt(T))
        mask = jax.random.uniform(k4, (O, T), dtype=jnp.float32)
        bias = jax.random.normal(k5, (O,), dtype=jnp.float32)
        return {'x': x, 'y': y, 'weight': weight, 'mask': mask, 'bias': bias}
    _L3_cond_all = _L3_cond_setup()
    _L3_cond_in = {k: v for k, v in _L3_cond_all.items() if k in ('weight', 'mask', 'bias')}
    del _L3_cond_all
    return {'x': x, 'cond_8': cond_8, 'L0_cond_W_base': _L0_cond_in['W_base'], 'L0_cond_b_base': _L0_cond_in['b_base'], 'L0_cond_As': _L0_cond_in['As'], 'L0_cond_Bs': _L0_cond_in['Bs'], 'L1_cond_skill_gate': _L1_cond_in['skill_gate'], 'L1_cond_skill_up': _L1_cond_in['skill_up'], 'L1_cond_skill_down': _L1_cond_in['skill_down'], 'L1_cond_shared_gate': _L1_cond_in['shared_gate'], 'L1_cond_shared_up': _L1_cond_in['shared_up'], 'L1_cond_shared_down': _L1_cond_in['shared_down'], 'L2_cond_W_up': _L2_cond_in['W_up'], 'L2_cond_b_up': _L2_cond_in['b_up'], 'L2_cond_W_gate': _L2_cond_in['W_gate'], 'L2_cond_b_gate': _L2_cond_in['b_gate'], 'L2_cond_W_down': _L2_cond_in['W_down'], 'L2_cond_b_down': _L2_cond_in['b_down'], 'L3_cond_weight': _L3_cond_in['weight'], 'L3_cond_mask': _L3_cond_in['mask'], 'L3_cond_bias': _L3_cond_in['bias']}

def reference(x, cond_8, L0_cond_W_base, L0_cond_b_base, L0_cond_As, L0_cond_Bs, L1_cond_skill_gate, L1_cond_skill_up, L1_cond_skill_down, L1_cond_shared_gate, L1_cond_shared_up, L1_cond_shared_down, L2_cond_W_up, L2_cond_b_up, L2_cond_W_gate, L2_cond_b_gate, L2_cond_W_down, L2_cond_b_down, L3_cond_weight, L3_cond_mask, L3_cond_bias):
    import jax
    import jax.numpy as jnp

    def _L0_cond_ref(x, w, W_base, b_base, As, Bs):
        import jax, jax.numpy as jnp
        import numpy as np
        R = 16
        ALPHA = 32.0
        SCALING = ALPHA / R
        out = jnp.einsum('btc,oc->bto', x, W_base) + b_base
        h = jnp.einsum('btc,erc->bter', x, As)
        lora = jnp.einsum('bter,eor,be->bto', h, Bs, w)
        return out + lora * SCALING

    def _L1_cond_ref(x, router_logits, skill_gate, skill_up, skill_down, shared_gate, shared_up, shared_down):
        import jax, jax.numpy as jnp
        import numpy as np
        TOP_K = 2
        NUM_MOE_LAYERS = 12

        def _gemma_mlp(x, gate_w, up_w, down_w):
            g = jnp.einsum('bsh,hi->bsi', x, gate_w)
            u = jnp.einsum('bsh,hi->bsi', x, up_w)
            return jnp.einsum('bsi,ih->bsh', jax.nn.gelu(g, approximate=True) * u, down_w)
        B = x.shape[0]
        E = skill_gate.shape[0]
        rw = jax.nn.softmax(router_logits.astype(jnp.float32), axis=-1)
        w, sel = jax.lax.top_k(rw, TOP_K)
        w = w / w.sum(axis=-1, keepdims=True)
        w = w.astype(x.dtype)
        scale = 1.0 / NUM_MOE_LAYERS
        w = scale * w + (1.0 - scale) * jax.lax.stop_gradient(w)
        dense_w = jnp.zeros((B, E), x.dtype).at[jnp.arange(B)[:, None], sel].add(w)

        def step(acc, params):
            g, u, d, we = params
            return (acc + we[:, None, None] * _gemma_mlp(x, g, u, d), None)
        out, _ = jax.lax.scan(step, jnp.zeros_like(x), (skill_gate, skill_up, skill_down, dense_w.T))
        out = out + _gemma_mlp(x, shared_gate, shared_up, shared_down)
        return out

    def _L2_cond_ref(x, opcode_onehot, W_up, b_up, W_gate, b_gate, W_down, b_down):
        import jax, jax.numpy as jnp
        import numpy as np
        B, S, D = (16, 512, 256)
        E, H = (8, 512)
        expert = jnp.argmax(opcode_onehot, axis=-1)
        wu, bu = (W_up[expert], b_up[expert])
        wg, bg = (W_gate[expert], b_gate[expert])
        wd, bd = (W_down[expert], b_down[expert])
        up = jnp.einsum('bsd,bhd->bsh', x, wu) + bu[:, None, :]
        gate = jnp.einsum('bsd,bhd->bsh', x, wg) + bg[:, None, :]
        hidden = jax.nn.silu(up) * gate
        out = jnp.einsum('bsh,bdh->bsd', hidden, wd) + bd[:, None, :]
        return out

    def _L3_cond_ref(x, y, weight, mask, bias):
        import jax, jax.numpy as jnp
        import numpy as np
        masked_w = weight * mask[None, :, :]
        w_bot = jnp.einsum('bg,got->bot', y, masked_w)
        return jnp.einsum('bnt,bot->bno', x, w_bot) + bias
    x = x + _L0_cond_ref(x, cond_8, L0_cond_W_base, L0_cond_b_base, L0_cond_As, L0_cond_Bs)
    x = x + _L1_cond_ref(x, cond_8, L1_cond_skill_gate, L1_cond_skill_up, L1_cond_skill_down, L1_cond_shared_gate, L1_cond_shared_up, L1_cond_shared_down)
    x = x + _L2_cond_ref(x, cond_8, L2_cond_W_up, L2_cond_b_up, L2_cond_W_gate, L2_cond_b_gate, L2_cond_W_down, L2_cond_b_down)
    x = x + _L3_cond_ref(x, cond_8, L3_cond_weight, L3_cond_mask, L3_cond_bias)
    return x

_drawn_inputs = setup_inputs


def setup_inputs(seed=0):
    import zlib

    import numpy as np

    out = dict(_drawn_inputs(seed))
    spreads = {'L2_cond_b_up': (0.0, 0.8), 'L2_cond_b_gate': (0.0, 0.8), 'L2_cond_b_down': (0.0, 0.1)}
    factors = {'L0_cond_b_base': 4.201, 'L1_cond_skill_gate': 2.719, 'L2_cond_W_up': 2.674}
    for name, (base, spread) in spreads.items():
        noise = np.random.default_rng([zlib.crc32(name.encode()), seed]).standard_normal(out[name].shape)
        drawn = base * np.exp(spread * noise) if base else spread * noise
        out[name] = jnp.asarray(drawn.astype(out[name].dtype))
    for name, factor in factors.items():
        out[name] = (out[name] * factor).astype(out[name].dtype)
    return out
```

```python
from contextlib import ExitStack

import numpy as np

import concourse.bass as bass
from concourse import mybir

ALU = mybir.AluOpType
ACT = mybir.ActivationFunctionType
AX_X = mybir.AxisListType.X
F32 = mybir.dt.float32
F32R = mybir.dt.float32r
I32 = mybir.dt.int32
U32 = mybir.dt.uint32
ds = bass.ds

P = 128
NB, TOK, D = 64, 64, 256
NE = 8
KD = D // P
BLK = 4
BT = BLK * TOK
CH = 2 * BT
I1 = 1024
H2 = 512
STEPH = 256
WCOL = 3 * CH
RAWS = 4
N_SHARED = NB // BLK
N_TOP2 = (2 * NB + NE * (BLK - 1)) // BLK
N_TOP1 = (NB + NE * (BLK - 1)) // BLK
SLOTS1, SLOTS2 = N_TOP2 * BLK, N_TOP1 * BLK
assert N_SHARED % 2 == 0 and N_TOP2 % 2 == 0 and N_TOP1 % 2 == 0
assert I1 == 4 * STEPH and H2 == 2 * STEPH
R_LORA = 16
SCALING = 2.0
N_TILE0 = NB // BLK
N_TILE3 = NB // 2


def wait(eng, sem, value):
    if not isinstance(value, int) or value > 0:
        eng.wait_ge(sem, value)


def rounds(eng, n, body):
    body(0, False)
    with eng.Fori(1, n - 1) as i:
        body(i, False)
    body(n - 1, True)


def build(nc, x, cond, w_base, b_base, a_lora, b_lora, gate1, up1, down1, sgate, sup, sdown,
          up2, bup2, gate2, bgate2, down2, bdown2, weight3, mask3, bias3, out):
    x_tok = x.rearrange("b t c -> (b t) c")
    out_tok = out.rearrange("b t c -> (b t) c")
    w2t = nc.dram_tensor("w2t", (NE, P, 2 * WCOL), F32, kind="Internal").ap()

    with ExitStack() as ctx:
        def sb(name, shape, dt=F32):
            return ctx.enter_context(nc.sbuf_tensor(name, shape, dt))

        def sem(name):
            return ctx.enter_context(nc.semaphore(name))

        mem = dict(
            acc=sb("acc", [P, NB, KD, TOK]),
            xhl=sb("xhl", [P, NB, 2 * KD, TOK], F32R),
            w3hl=sb("w3hl", [P, 2, KD, NE, D], F32R),
            raw=sb("raw", [P, RAWS, WCOL]),
            whl=sb("whl", [P, 2, 2, WCOL], F32R),
            xg=sb("xg", [P, 2, 2 * KD, BT], F32R),
            gel=sb("gel", [P, 2, CH]),
            act=sb("act", [P, 2, CH]),
            ahl=sb("ahl", [P, 2, 2, CH], F32R),
            ident=sb("ident", [P, P]),
            wslot1=sb("wslot1", [P, SLOTS1]),
            wslot2=sb("wslot2", [P, SLOTS2]),
            bslot1=sb("bslot1", [1, SLOTS1], I32),
            bslot2=sb("bslot2", [1, SLOTS2], I32),
            eblk1=sb("eblk1", [1, N_TOP2], I32),
            eblk2=sb("eblk2", [1, N_TOP1], I32),
            btab=sb("btab", [P, NBIAS]),
            bdn_b=sb("bdn_b", [P, NB, KD]),
            wexp=sb("wexp", [P, NB]),
            ytab=sb("ytab", [P, N_TILE3, NE]),
            bias3_b=sb("bias3_b", [P, D]),
        )
        banks = [ctx.enter_context(nc.psum_tensor(f"bank{i}", [P, CH], F32)) for i in range(8)]

        prepare(nc, sem, mem, banks, cond, b_base, up2, bup2, gate2, bgate2, down2, bdown2,
                weight3, mask3, bias3, w2t)
        layer0(nc, sem, mem, banks, x_tok, w_base, a_lora, b_lora)
        mlp(nc, sem, mem, banks, 1, (gate1, up1, down1), (sgate, sup, sdown))
        mlp(nc, sem, mem, banks, 2, w2t, None)
        layer3(nc, sem, mem, banks, out_tok)


NBIAS = 2 * NE * 4 + KD


def prepare(nc, sem, mem, banks, cond, b_base, up2, bup2, gate2, bgate2, down2, bdown2,
            weight3, mask3, bias3, w2t):
    gel, w3hl, ident = mem["gel"], mem["w3hl"], mem["ident"]
    nat = mem["raw"][:, :, :].rearrange("p s w -> p (s w)")
    acc = mem["acc"][:, :, :, :].rearrange("p b k t -> p (b k t)")
    stage = acc[:, 0:4 * WCOL]
    maskn = mem["act"][:, 0, :]
    at = [4 * WCOL]

    def rb(parts, *shape, dt=F32):
        n = int(np.prod(shape))
        view = acc[0:parts, at[0]:at[0] + n]
        at[0] += n
        assert at[0] <= NB * KD * TOK
        if dt is not F32:
            view = view.bitcast(dt)
        if len(shape) == 2:
            view = view.rearrange("p (a b) -> p a b", a=shape[0])
        if len(shape) == 3:
            view = view.rearrange("p (a b c) -> p a b c", a=shape[0], b=shape[1])
        return view

    cnd = rb(NB, NE)
    top = rb(NB, 8)
    topi = rb(NB, 8, dt=U32)
    topf = rb(NB, 8)
    ntop = rb(NB, 1)
    ex = rb(NB, 8)
    prob = rb(NB, 12)
    hot = rb(NB, 3, NE)
    iota_e = rb(NB, NE)
    tri = rb(NB, NB)
    ones = rb(NB, P)
    iota_b = rb(NB, P)
    iota_s = rb(NB, SLOTS1)
    icnt = rb(P, 2, NE, dt=I32)
    run = rb(P, 3, 2, NE)
    first = rb(P, 2, NE)
    pos = rb(NB, 2, NE)
    hpos = rb(NB, 3, NE)
    slot_of = rb(NB, 3)
    onehot = rb(NB, 2 * SLOTS1 + SLOTS2)
    wb = rb(NB, 2, P)
    hotT = rb(NE, NB)
    cexp = rb(NB, NE, R_LORA)
    bnat = rb(NBIAS, P)
    bdn_n = mem["act"][0:NE, 1, 0:D]
    iota4 = rb(1, N_TOP2)
    ended = mem["act"][0:1, 1, D:D + N_TOP1 * NE].rearrange("p (j e) -> p j e", e=NE)
    n_ended = rb(1, N_TOP2)
    HALF = N_TOP2 // 2
    assert HALF <= N_TOP1

    s_const = sem("s_const")
    s_cond = sem("s_cond")
    s_small = sem("s_small")
    s_route = sem("s_route")
    s_exp = sem("s_exp")
    s_sel = sem("s_sel")
    s_nat2 = [sem(f"s_nat2_{u}") for u in range(2)]
    s_nat3 = [sem(f"s_nat3_{u}") for u in range(2)]
    s_tr2 = sem("s_tr2")
    s_tr3 = sem("s_tr3")
    s_masked = sem("s_masked")
    s_ev_act = sem("s_ev_act")
    s_ev_dve = sem("s_ev_dve")
    s_w3hi = sem("s_w3hi")
    s_w3lo = sem("s_w3lo")
    s_w2t = [sem(f"s_w2t_{u}") for u in range(2)]
    mark = {}

    with nc.Block() as block:
        @block.sync
        def _(sp):
            sp.dma_start(cnd, cond).then_inc(s_cond, 16)
            n_small = 0
            for dst, src in (
                (maskn.rearrange("p (c t) -> p c t", c=KD), mask3.rearrange("(c p) t -> p c t", p=P)),
                (bdn_n, bdown2),
                (bnat[0:32, :], bup2.rearrange("e (c p) -> (e c) p", p=P)),
                (bnat[32:64, :], bgate2.rearrange("e (c p) -> (e c) p", p=P)),
                (bnat[64:NBIAS, :], b_base.rearrange("(c p) -> c p", p=P)),
                (mem["bias3_b"][:, :], bias3.rearrange("(a n) -> a n", a=1).broadcast_to([P, D])),
                (mem["ytab"][0:TOK, :, :],
                 cond.rearrange("(t h) e -> h t e", h=2)[0:1].broadcast_to([TOK, N_TILE3, NE])),
                (mem["ytab"][TOK:P, :, :],
                 cond.rearrange("(t h) e -> h t e", h=2)[1:2].broadcast_to([TOK, N_TILE3, NE])),
            ):
                sp.dma_start(dst, src).then_inc(s_small, 16)
                n_small += 16
            mark["small"] = n_small

            def load(e, u):
                o = u * 2 * WCOL
                wait(sp, s_tr2, 6 * (e - 1))
                for k, w in enumerate((up2, gate2)):
                    sp.dma_start(nat[:, o + k * 1024:o + (k + 1) * 1024].rearrange("p (c d) -> p c d", d=D),
                                 w[ds(e, 1)].rearrange("e (c p) d -> p (e c) d", p=P)).then_inc(s_nat2[u], 16)
                sp.dma_start(nat[:, o + 2048:o + 3072].rearrange("p (c h) -> p c h", h=H2),
                             down2[ds(e, 1)].rearrange("e (c p) h -> p (e c) h", p=P)).then_inc(s_nat2[u], 16)
                wait(sp, s_tr3, e - 1)
                sp.dma_start(gel[:, u, :].rearrange("p (c t) -> p c t", t=D),
                             weight3[ds(e, 1)].rearrange("e (c p) t -> p (e c) t", p=P)).then_inc(s_nat3[u], 16)

            load(0, 0)
            load(1, 1)

            def pair(i, last):
                for u in range(2):
                    e = 2 * i + u
                    sp.wait_ge(s_ev_act, 3 * (e + 1))
                    sp.wait_ge(s_ev_dve, 3 * (e + 1))
                    sp.dma_start(w2t[ds(e, 1)].rearrange("e p w -> p (e w)"),
                                 stage[:, u * 2 * WCOL:(u + 1) * 2 * WCOL]).then_inc(s_w2t[u], 16)
                    if not last:
                        load(e + 2, u)

            rounds(sp, NE // 2, pair)
            for u in range(2):
                sp.wait_ge(s_w2t[u], 16 * (NE // 2))

        @block.gpsimd
        def _(pool):
            pool.memset(ident[:, :], 0.0).then_inc(s_const, 1)
            pool.memset(tri, 0.0).then_inc(s_const, 1)
            pool.memset(ones, 1.0).then_inc(s_const, 1)
            for dst, pattern, channel in ((iota_e, [[1, NE]], 0), (iota_b, [[0, P]], 1),
                                          (iota_s, [[1, SLOTS1]], 0), (iota4, [[BLK, N_TOP2]], 0)):
                pool.iota(dst, pattern, base=0, channel_multiplier=channel,
                          allow_small_or_imprecise_dtypes=True).then_inc(s_const, 1)
            pool.wait_ge(s_const, 7)
            pool.affine_select(out=ident[:, :], in_=ident[:, :], compare_op=ALU.not_equal, fill=1.0,
                               base=0, pattern=[[-1, P]], channel_multiplier=1).then_inc(s_const, 1)
            pool.affine_select(out=tri, in_=tri, compare_op=ALU.is_ge, fill=1.0,
                               base=0, pattern=[[-1, NB]], channel_multiplier=1).then_inc(s_const, 1)

        @block.vector
        def _(dve):
            steps = [0]

            def step(ins):
                steps[0] += 1
                ins.then_inc(s_route, 1)
                dve.wait_ge(s_route, steps[0])

            dve.wait_ge(s_cond, 16)
            dve.wait_ge(s_const, 9)
            step(nc.vector.max(top, cnd))
            step(nc.vector.max_index(topi, top, cnd))
            step(nc.vector.tensor_copy(topf, topi))
            step(nc.vector.tensor_scalar(ntop, top[:, 0:1], -1.0, None, ALU.mult))
            mark["ntop"] = steps[0]
            for k in range(2):
                step(nc.vector.tensor_scalar(hot[:, k, :], iota_e, topf[:, k:k + 1], None, ALU.is_equal))
            step(nc.vector.tensor_tensor(hot[:, 2, :], hot[:, 0, :], hot[:, 1, :], ALU.add))
            mark["hot"] = steps[0]
            dve.wait_ge(s_exp, 1)
            step(nc.vector.reduce_sum(prob[:, 0:1], ex, AX_X))
            step(nc.vector.reciprocal(prob[:, 1:2], prob[:, 0:1]))
            step(nc.vector.tensor_scalar(prob[:, 2:4], ex[:, 0:2], prob[:, 1:2], None, ALU.mult))
            step(nc.vector.tensor_tensor(prob[:, 4:5], prob[:, 2:3], prob[:, 3:4], ALU.add))
            step(nc.vector.reciprocal(prob[:, 5:6], prob[:, 4:5]))
            step(nc.vector.tensor_scalar(prob[:, 6:8], prob[:, 2:4], prob[:, 5:6], None, ALU.mult))
            step(nc.vector.tensor_scalar(prob[:, 8:10], prob[:, 6:8], 1.0 - 1.0 / 12, None, ALU.mult))
            step(nc.vector.scalar_tensor_tensor(prob[:, 10:12], prob[:, 6:8], 1.0 / 12, prob[:, 8:10],
                                                ALU.mult, ALU.add))
            for k in range(2):
                step(nc.vector.tensor_scalar(wb[:, k, :], ones, prob[:, 10 + k:11 + k], None, ALU.mult))
            dve.wait_ge(s_sel, 1)
            counts = banks[7][:, 16:32].rearrange("p (a e) -> p a e", a=2)
            step(nc.vector.tensor_scalar(icnt, counts, float(BLK - 1), None, ALU.add))
            step(nc.vector.tensor_scalar(icnt, icnt, BLK.bit_length() - 1, BLK.bit_length() - 1,
                                         ALU.logical_shift_right, ALU.logical_shift_left))
            step(nc.vector.tensor_copy(run[:, 0], icnt))
            for shift, a, b in ((1, 0, 1), (2, 1, 2), (4, 2, 1)):
                step(nc.vector.tensor_copy(run[:, b, :, 0:shift], run[:, a, :, 0:shift]))
                step(nc.vector.tensor_tensor(run[:, b, :, shift:], run[:, a, :, shift:],
                                             run[:, a, :, :NE - shift], ALU.add))
            end = run[:, 1]
            step(nc.vector.tensor_tensor(first, end, run[:, 0], ALU.subtract))
            rank = banks[7][:NB, 0:16].rearrange("p (a e) -> p a e", a=2)
            step(nc.vector.tensor_tensor(pos, rank, first[:NB], ALU.add))
            for k in range(2):
                step(nc.vector.tensor_tensor(hpos[:, k, :], hot[:, k, :], pos[:, 0, :], ALU.mult))
            step(nc.vector.tensor_tensor(hpos[:, 2, :], hot[:, 0, :], pos[:, 1, :], ALU.mult))
            step(nc.vector.reduce_sum(slot_of, hpos, AX_X))
            for k in range(3):
                width = SLOTS1 if k < 2 else SLOTS2
                step(nc.vector.tensor_scalar(onehot[:, k * SLOTS1:k * SLOTS1 + width], iota_s[:, :width],
                                             slot_of[:, k:k + 1], None, ALU.is_equal))
            step(nc.vector.tensor_copy(cexp, cnd.unsqueeze(2).broadcast_to([NB, NE, R_LORA])))
            mark["onehot"] = steps[0]
            for a, j0, n, tab in ((0, 0, HALF, "eblk1"), (0, HALF, HALF, "eblk1"), (1, 0, N_TOP1, "eblk2")):
                step(nc.vector.tensor_tensor(ended[:, :n, :],
                                             iota4[:, j0:j0 + n].unsqueeze(2).broadcast_to([1, n, NE]),
                                             end[0:1, a, :].unsqueeze(1).broadcast_to([1, n, NE]), ALU.is_ge))
                step(nc.vector.reduce_sum(n_ended[:, :n], ended[:, :n, :], AX_X))
                step(nc.vector.tensor_scalar(mem[tab][:, j0:j0 + n], n_ended[:, :n], float(NE - 1), None,
                                             ALU.min))
            b7 = banks[7]
            dve.wait_ge(s_sel, 2)
            step(nc.vector.tensor_copy(mem["wslot1"][:, :], b7[:, 0:SLOTS1]))
            step(nc.vector.tensor_copy(mem["bslot1"][:, :], b7[0:1, 160:160 + SLOTS1]))
            step(nc.vector.tensor_copy(mem["wslot2"][:, :], b7[:, 320:320 + SLOTS2]))
            step(nc.vector.tensor_copy(mem["bslot2"][:, :], b7[0:1, 416:416 + SLOTS2]))
            mark["tables"] = steps[0]
            dve.wait_ge(s_sel, 3)
            step(nc.vector.tensor_copy(hotT, b7[:NE, 0:NB]))
            step(nc.vector.tensor_scalar(mem["wexp"][:, :], b7[:, 64:128], SCALING, None, ALU.mult))
            step(nc.vector.tensor_copy(mem["btab"][:, :], b7[:, 128:128 + NBIAS]))
            mark["hotT"] = steps[0]
            dve.wait_ge(s_sel, 4)
            step(nc.vector.tensor_copy(mem["bdn_b"][:, :, :],
                                       b7[:, 0:KD * NB].rearrange("p (k b) -> p b k", k=KD)))
            dve.wait_ge(s_small, mark["small"])

            def pair(i, last):
                for u in range(2):
                    e = 2 * i + u
                    dve.wait_ge(s_nat3[u], 16 * (i + 1))
                    nc.vector.tensor_tensor(gel[:, u, :], gel[:, u, :], maskn, ALU.mult).then_inc(s_masked, 1)
                    for m in (1, 3, 5):
                        dve.wait_ge(s_tr2, 6 * e + m + 1)
                        if m == 1:
                            wait(dve, s_w2t[u], 16 * i)
                        o = u * 2 * WCOL + m * CH
                        nc.vector.tensor_copy(stage[:, o:o + CH], banks[m][:, :]).then_inc(s_ev_dve, 1)
                    dve.wait_ge(s_w3hi, e + 1)
                    hi = w3hl[:, 0, :, ds(e, 1), :].rearrange("p k e o -> p k (e o)").bitcast(F32)
                    lo = w3hl[:, 1, :, ds(e, 1), :].rearrange("p k e o -> p k (e o)")
                    nc.vector.tensor_tensor(lo, banks[6][:, :].rearrange("p (k o) -> p k o", k=KD), hi,
                                            ALU.subtract).then_inc(s_w3lo, 1)

            rounds(dve, NE // 2, pair)

        @block.scalar
        def _(se):
            se.wait_ge(s_route, mark["ntop"])
            se.activation(ex, top, ACT.Exp, bias=ntop[:, 0:1]).then_inc(s_exp, 1)

            def pair(i, last):
                for u in range(2):
                    e = 2 * i + u
                    for m in (0, 2, 4):
                        se.wait_ge(s_tr2, 6 * e + m + 1)
                        if m == 0:
                            wait(se, s_w2t[u], 16 * i)
                        o = u * 2 * WCOL + m * CH
                        se.activation(stage[:, o:o + CH], banks[m][:, :], ACT.Copy).then_inc(s_ev_act, 1)
                    se.wait_ge(s_tr3, e + 1)
                    se.activation(w3hl[:, 0, :, ds(e, 1), :].rearrange("p k e o -> p k (e o)"),
                                  banks[6][:, :].rearrange("p (k o) -> p k o", k=KD),
                                  ACT.Copy).then_inc(s_w3hi, 1)

            rounds(se, NE // 2, pair)

        @block.tensor
        def _(pe):
            b7 = banks[7]
            mm = nc.tensor.matmul
            pe.wait_ge(s_const, 9)
            pe.wait_ge(s_route, mark["hot"])
            mm(b7[:NB, 0:8], tri, hot[:, 2, :], start=True, stop=True)
            mm(b7[:NB, 8:16], tri, hot[:, 0, :], start=True, stop=True)
            mm(b7[:, 16:24], ones, hot[:, 2, :], start=True, stop=True)
            mm(b7[:, 24:32], ones, hot[:, 0, :], start=True, stop=True).then_inc(s_sel, 1)
            pe.wait_ge(s_route, mark["onehot"])
            for lhs, o in (((wb[:, 0, :], wb[:, 1, :]), 0), ((iota_b, iota_b), 160)):
                for k in range(2):
                    mm(b7[:, o:o + SLOTS1], lhs[k], onehot[:, k * SLOTS1:(k + 1) * SLOTS1],
                       start=k == 0, stop=k == 1)
            for lhs, o in ((ones, 320), (iota_b, 416)):
                last = mm(b7[:, o:o + SLOTS2], lhs, onehot[:, 2 * SLOTS1:], start=True, stop=True)
            last.then_inc(s_sel, 1)
            pe.wait_ge(s_route, mark["tables"])
            pe.wait_ge(s_small, mark["small"])
            nc.tensor.transpose(b7[:NE, 0:NB], hot[:, 0, :], ident[:NB, :NB])
            mm(b7[:, 64:128], cexp.rearrange("b e r -> b (e r)"), ident[:NB, :NB], start=True, stop=True)
            nc.tensor.transpose(b7[:, 128:128 + NBIAS], bnat, ident[:NBIAS, :NBIAS]).then_inc(s_sel, 1)
            pe.wait_ge(s_route, mark["hotT"])
            for k in range(KD):
                last = mm(b7[:, k * NB:(k + 1) * NB], bdn_n[:, k * P:(k + 1) * P], hotT, start=True, stop=True)
            last.then_inc(s_sel, 1)

            def pair(i, last):
                for u in range(2):
                    e = 2 * i + u
                    o = u * 2 * WCOL
                    pe.wait_ge(s_nat2[u], 48 * (i + 1))
                    for m in range(6):
                        s, part = divmod(m, 3)
                        wait(pe, (s_ev_act, s_ev_dve)[m % 2], 3 * (e - 1) + m // 2 + 1)
                        for a in range(2):
                            for c in range(2):
                                if part < 2:
                                    q = o + part * 1024 + (2 * s + c) * D + a * P
                                else:
                                    q = o + 2048 + c * H2 + (2 * s + a) * P
                                t = nc.tensor.transpose(banks[m][:, a * D + c * P:a * D + (c + 1) * P],
                                                        nat[:, q:q + P], ident[:, :])
                        t.then_inc(s_tr2, 1)
                    pe.wait_ge(s_masked, e + 1)
                    wait(pe, s_w3lo, e)
                    for k in range(KD):
                        for c in range(KD):
                            q = c * D + k * P
                            t = nc.tensor.transpose(banks[6][:, k * D + c * P:k * D + (c + 1) * P],
                                                    gel[:, u, q:q + P], ident[:, :])
                    t.then_inc(s_tr3, 1)

            rounds(pe, NE // 2, pair)


def split3(mm, out, w_hi, w_lo, x_hi, x_lo, start, stop, **kw):
    mm(out, w_lo, x_hi, start=start, stop=False, **kw)
    mm(out, w_hi, x_lo, start=False, stop=False, **kw)
    return mm(out, w_hi, x_hi, start=False, stop=stop, **kw)


def layer0(nc, sem, mem, banks, x_tok, w_base, a_lora, b_lora):
    raw, whl, xg, ahl, acc, xhl = (mem[k] for k in ("raw", "whl", "xg", "ahl", "acc", "xhl"))
    ident, btab, wexp = mem["ident"], mem["btab"], mem["wexp"]
    W_OFF, A_OFF, B_OFF, L0W = 0, CH, CH + D, 2 * CH
    x_in = [raw[:, 1, u * CH:(u + 1) * CH].rearrange("p (s c) -> p s c", c=D) for u in range(2)]
    x0f = [raw[:, 2, u * CH:(u + 1) * CH] for u in range(2)]
    hs = [raw[:, 3, u * BT:(u + 1) * BT] for u in range(2)]
    x0hl = [xg[:, u, :, :] for u in range(2)]
    hshl = [ahl[:, u, :, 0:BT] for u in range(2)]
    ps_x, ps_h, ps_y = banks[2:4], banks[4:6], banks[6:8]

    s_w0 = sem("s_w0")
    s_w0t = sem("s_w0t")
    s_w0hi = sem("s_w0hi")
    s_w0lo = sem("s_w0lo")
    s_xin = [sem(f"s_xin_{u}") for u in range(2)]
    s_xt = sem("s_xt")
    s_x0hi = sem("s_x0hi")
    s_x0lo = sem("s_x0lo")
    s_h = sem("s_h")
    s_hs = sem("s_hs")
    s_hshi = sem("s_hshi")
    s_hslo = sem("s_hslo")
    s_y = sem("s_y")
    s_x1 = sem("s_x1")
    s_x1hi = sem("s_x1hi")

    with nc.Block() as block:
        @block.sync
        def _(sp):
            nat = raw[:, 0, :]
            sp.dma_start(nat[:, 0:CH].rearrange("p (c n) -> p c n", c=KD),
                         w_base.rearrange("(c p) n -> p c n", p=P)).then_inc(s_w0, 16)
            sp.dma_start(nat[:, CH:CH + D], a_lora.rearrange("e r c -> (e r) c")).then_inc(s_w0, 16)
            for c in range(KD):
                sp.dma_start(nat[:, CH + D + c * P:CH + D + (c + 1) * P].rearrange("p (e r) -> p e r", e=NE),
                             b_lora[:, c * P:(c + 1) * P, :].rearrange("e p r -> p e r")).then_inc(s_w0, 16)

            def pair(i, last):
                for u in range(2):
                    t = 2 * i + u
                    wait(sp, s_xt, t - 1)
                    sp.dma_start(x_in[u], x_tok[ds(t * BT, BT), :].rearrange("(s p) c -> p s c", p=P))\
                        .then_inc(s_xin[u], 16)

            rounds(sp, N_TILE0 // 2, pair)

        @block.tensor
        def _(pe):
            mm = nc.tensor.matmul
            nat = raw[:, 0, :]
            pe.wait_ge(s_w0, 64)
            for k in range(KD):
                for c in range(KD):
                    nc.tensor.transpose(banks[0][:, k * D + c * P:k * D + (c + 1) * P],
                                        nat[:, c * D + k * P:c * D + (k + 1) * P], ident[:, :])
                nc.tensor.transpose(banks[1][:, k * P:(k + 1) * P], nat[:, CH + k * P:CH + (k + 1) * P],
                                    ident[:, :])
            for c in range(KD):
                t = nc.tensor.transpose(banks[1][:, D + c * P:D + (c + 1) * P],
                                        nat[:, CH + D + c * P:CH + D + (c + 1) * P], ident[:, :])
            t.then_inc(s_w0t, 1)

            def w(hl, o):
                return whl[:, 0, hl, o:o + P]

            def transposes(t, u, n):
                pe.wait_ge(s_xin[u], 16 * n)
                wait(pe, s_x0hi, t - 1)
                for s in range(2):
                    for k in range(KD):
                        last = nc.tensor.transpose(ps_x[u][:, k * BT + s * P:k * BT + (s + 1) * P],
                                                   x_in[u][:, s, k * P:(k + 1) * P], ident[:, :])
                last.then_inc(s_xt, 1)

            transposes(0, 0, 1)
            pe.wait_ge(s_w0lo, 2)

            def pair(i, last):
                for u in range(2):
                    t = 2 * i + u
                    if not (last and u == 1):
                        transposes(t + 1, 1 - u, i + 1 + u)
                    pe.wait_ge(s_x0lo, t + 1)
                    wait(pe, s_hs, t - 1)
                    for k in range(KD):
                        o = A_OFF + k * P
                        m = split3(mm, ps_h[u][:, 0:BT], w(0, o), w(1, o), x0hl[u][:, k, :], x0hl[u][:, KD + k, :],
                                   start=k == 0, stop=k == KD - 1)
                    m.then_inc(s_h, 1)
                    wait(pe, s_x1, t - 1)
                    for c in range(KD):
                        for k in range(KD):
                            o = W_OFF + k * D + c * P
                            split3(mm, ps_y[u][:, c * BT:(c + 1) * BT], w(0, o), w(1, o), x0hl[u][:, k, :],
                                   x0hl[u][:, KD + k, :], start=c == 0 and k == 0, stop=False,
                                   skip_group_check=True)
                    pe.wait_ge(s_hslo, t + 1)
                    for c in range(KD):
                        o = B_OFF + c * P
                        m = split3(mm, ps_y[u][:, c * BT:(c + 1) * BT], w(0, o), w(1, o), hshl[u][:, 0, :],
                                   hshl[u][:, 1, :], start=False, stop=True, skip_group_check=True)
                    m.then_inc(s_y, 1)

            rounds(pe, N_TILE0 // 2, pair)

        @block.scalar
        def _(se):
            se.wait_ge(s_w0t, 1)
            for b in range(2):
                se.activation(whl[:, 0, 0, b * CH:(b + 1) * CH], banks[b][:, :], ACT.Copy).then_inc(s_w0hi, 1)

            def tile_in(t, u):
                se.wait_ge(s_xt, t + 1)
                wait(se, s_x1, t - 1)
                se.activation(x0f[u], ps_x[u][:, :], ACT.Copy)
                wait(se, s_y, t - 1)
                se.activation(x0hl[u][:, 0:KD, :], ps_x[u][:, :].rearrange("p (k t) -> p k t", k=KD),
                              ACT.Copy).then_inc(s_x0hi, 1)

            tile_in(0, 0)

            def pair(i, last):
                for u in range(2):
                    t = 2 * i + u
                    if not (last and u == 1):
                        tile_in(t + 1, 1 - u)
                    se.wait_ge(s_hs, t + 1)
                    wait(se, s_y, t - 1)
                    se.activation(hshl[u][:, 0, :], hs[u], ACT.Copy).then_inc(s_hshi, 1)
                    se.wait_ge(s_x1, t + 1)
                    se.activation(xhl[:, ds(t * BLK, BLK), 0:KD, :], acc[:, ds(t * BLK, BLK), :, :],
                                  ACT.Copy).then_inc(s_x1hi, 1)

            rounds(se, N_TILE0 // 2, pair)

        @block.vector
        def _(dve):
            for b in range(2):
                dve.wait_ge(s_w0hi, b + 1)
                nc.vector.tensor_tensor(whl[:, 0, 1, b * CH:(b + 1) * CH], banks[b][:, :],
                                        whl[:, 0, 0, b * CH:(b + 1) * CH].bitcast(F32),
                                        ALU.subtract).then_inc(s_w0lo, 1)

            def tile_in(t, u):
                dve.wait_ge(s_x0hi, t + 1)
                nc.vector.tensor_tensor(x0hl[u][:, KD:, :], x0f[u].rearrange("p (k t) -> p k t", k=KD),
                                        x0hl[u][:, 0:KD, :].bitcast(F32), ALU.subtract).then_inc(s_x0lo, 1)

            tile_in(0, 0)

            def pair(i, last):
                for u in range(2):
                    t = 2 * i + u
                    if not (last and u == 1):
                        tile_in(t + 1, 1 - u)
                    dve.wait_ge(s_h, t + 1)
                    w = wexp[:, ds(t * BLK, BLK)].unsqueeze(2).broadcast_to([P, BLK, TOK])
                    nc.vector.tensor_tensor(hs[u].rearrange("p (b t) -> p b t", b=BLK),
                                            ps_h[u][:, 0:BT].rearrange("p (b t) -> p b t", b=BLK), w,
                                            ALU.mult).then_inc(s_hs, 1)
                    dve.wait_ge(s_hshi, t + 1)
                    nc.vector.tensor_tensor(hshl[u][:, 1, :], hs[u], hshl[u][:, 0, :].bitcast(F32),
                                            ALU.subtract).then_inc(s_hslo, 1)
                    dve.wait_ge(s_y, t + 1)
                    for c in range(KD):
                        m = nc.vector.scalar_tensor_tensor(
                            acc[:, ds(t * BLK, BLK), c, :],
                            ps_y[u][:, c * BT:(c + 1) * BT].rearrange("p (b t) -> p b t", b=BLK),
                            btab[:, 2 * NE * 4 + c:2 * NE * 4 + c + 1],
                            x0f[u][:, c * BT:(c + 1) * BT].rearrange("p (b t) -> p b t", b=BLK),
                            ALU.add, ALU.add)
                    m.then_inc(s_x1, 1)
                    dve.wait_ge(s_x1hi, t + 1)
                    nc.vector.tensor_tensor(xhl[:, ds(t * BLK, BLK), KD:, :], acc[:, ds(t * BLK, BLK), :, :],
                                            xhl[:, ds(t * BLK, BLK), 0:KD, :].bitcast(F32), ALU.subtract)

            rounds(dve, N_TILE0 // 2, pair)


RESPLIT = 8


def resplit_hi(nc, se, mem, s_hi):
    n = NB // RESPLIT
    for c in range(RESPLIT):
        se.activation(mem["xhl"][:, c * n:(c + 1) * n, 0:KD, :], mem["acc"][:, c * n:(c + 1) * n, :, :],
                      ACT.Copy).then_inc(s_hi, 1)


def resplit_lo(nc, dve, mem, s_hi, s_lo):
    n = NB // RESPLIT
    for c in range(RESPLIT):
        dve.wait_ge(s_hi, c + 1)
        nc.vector.tensor_tensor(mem["xhl"][:, c * n:(c + 1) * n, KD:, :], mem["acc"][:, c * n:(c + 1) * n, :, :],
                                mem["xhl"][:, c * n:(c + 1) * n, 0:KD, :].bitcast(F32),
                                ALU.subtract).then_inc(s_lo, 1)


def mlp(nc, sem, mem, banks, layer, weights, shared):
    raw, whl, xg, gel, act, ahl = (mem[k] for k in ("raw", "whl", "xg", "gel", "act", "ahl"))
    acc, xhl, btab = mem["acc"], mem["xhl"], mem["btab"]
    wslot, bslot, eblk = mem[f"wslot{layer}"], mem[f"bslot{layer}"], mem[f"eblk{layer}"]
    spb = 4 if layer == 1 else 2
    spi = 2 * spb
    n_sh = N_SHARED // 2 if shared else 0
    n_it = n_sh + (N_TOP2 if layer == 1 else N_TOP1) // 2
    ps_gate, ps_up, ps_out = banks[0:2], banks[2:4], banks[4:6]
    GU = 2 * CH
    per_load = 48 if layer == 1 else 16

    L = f"_{layer}"
    s_raw = [sem(f"s_raw{r}{L}") for r in range(RAWS)]
    s_whi = sem("s_whi" + L)
    s_wlo = sem("s_wlo" + L)
    s_dhi = sem("s_dhi" + L)
    s_dlo = sem("s_dlo" + L)
    s_xg = sem("s_xg" + L)
    s_gate = sem("s_gate" + L)
    s_up = sem("s_up" + L)
    s_gel = sem("s_gel" + L)
    s_act = sem("s_act" + L)
    s_ahi = sem("s_ahi" + L)
    s_alo = sem("s_alo" + L)
    s_dn = sem("s_dn" + L)
    s_acc = sem("s_acc" + L)
    s_xhi = sem("s_xhi" + L)
    s_xlo = sem("s_xlo" + L)

    def loop(eng, body):
        body(0, False, bool(n_sh), bool(n_sh))
        if n_sh:
            with eng.Fori(1, n_sh) as i:
                body(i, False, True, True)
            body(n_sh, False, True, False)
        with eng.Fori(n_sh + 1, n_it - 1) as i:
            body(i, False, False, False)
        body(n_it - 1, True, False, False)

    def turns(it, s):
        return it * (spi // RAWS) + s // RAWS + 1

    with nc.Block() as block:
        @block.sync
        def _(sp):
            def rounds_of(it, is_shared):
                for s in range(spi):
                    t = it * spi + s
                    if not is_shared and s % spb == 0:
                        e = sp.value_load(eblk[0:1, ds((it - n_sh) * 2 + s // spb, 1)],
                                          min_val=0, max_val=NE - 1)
                    wait(sp, s_wlo, t - RAWS + 1)
                    wait(sp, s_dlo, t - RAWS + 1)
                    dst, done = raw[:, s % RAWS, :], s_raw[s % RAWS]
                    q = s % spb
                    if layer == 2:
                        sp.dma_start(dst, weights[ds(e, 1), :, q * WCOL:(q + 1) * WCOL]
                                     .rearrange("e p w -> p (e w)")).then_inc(done, 16)
                        continue
                    for k in range(2):
                        if is_shared:
                            src = shared[k].rearrange("(c p) i -> p c i", p=P)
                        else:
                            src = weights[k][ds(e, 1)].rearrange("e (c p) i -> p (e c) i", p=P)
                        sp.dma_start(dst[:, k * CH:(k + 1) * CH].rearrange("p (c i) -> p c i", c=KD),
                                     src[:, :, q * STEPH:(q + 1) * STEPH]).then_inc(done, 16)
                    if is_shared:
                        src = shared[2][q * STEPH:(q + 1) * STEPH, :].rearrange("(c p) d -> p c d", p=P)
                    else:
                        src = weights[2][ds(e, 1), q * STEPH:(q + 1) * STEPH, :]\
                            .rearrange("e (c p) d -> p (e c) d", p=P)
                    sp.dma_start(dst[:, GU:].rearrange("p (c d) -> p c d", c=2), src).then_inc(done, 16)

            rounds_of(0, bool(n_sh))
            if n_sh:
                with sp.Fori(1, n_sh) as i:
                    rounds_of(i, True)
                with sp.Fori(n_sh, n_it) as i:
                    rounds_of(i, False)
            else:
                with sp.Fori(1, n_it) as i:
                    rounds_of(i, False)

        @block.gpsimd
        def _(pool):
            if layer == 2:
                pool.wait_ge(s_xlo, RESPLIT)

            def gather(it, is_shared):
                for u in range(2):
                    b = it * 2 + u
                    wait(pool, s_up, spb * (b - 1))
                    if is_shared:
                        pool.tensor_copy(xg[:, u, :, :].rearrange("p k (b t) -> p k b t", b=BLK),
                                         xhl[:, ds(b * BLK, BLK), :, :].rearrange("p b k t -> p k b t"))\
                            .then_inc(s_xg, BLK)
                        continue
                    for j in range(BLK):
                        batch = pool.value_load(bslot[0:1, ds((b - 2 * n_sh) * BLK + j, 1)],
                                                min_val=0, max_val=NB - 1)
                        pool.tensor_copy(xg[:, u, :, j * TOK:(j + 1) * TOK],
                                         xhl[:, ds(batch, 1), :, :].rearrange("p b k t -> p (b k) t"))\
                            .then_inc(s_xg, 1)

            gather(0, bool(n_sh))
            if n_sh:
                with pool.Fori(1, n_sh) as i:
                    gather(i, True)
                with pool.Fori(n_sh, n_it) as i:
                    gather(i, False)
            else:
                with pool.Fori(1, n_it) as i:
                    gather(i, False)

        @block.tensor
        def _(pe):
            mm = nc.tensor.matmul

            def project(it, s):
                t, p, u = it * spi + s, s % 2, s // spb
                if s % spb == 0:
                    pe.wait_ge(s_xg, BLK * (it * 2 + u + 1))
                pe.wait_ge(s_wlo, t + 1)
                for o, bank, freed, done in ((0, ps_gate[p], s_gel, s_gate), (CH, ps_up[p], s_act, s_up)):
                    wait(pe, freed, t - 1)
                    for c in range(2):
                        for k in range(KD):
                            q = o + k * STEPH + c * P
                            m = split3(mm, bank[:, c * BT:(c + 1) * BT], whl[:, p, 0, q:q + P],
                                       whl[:, p, 1, q:q + P], xg[:, u, k, :], xg[:, u, KD + k, :],
                                       start=k == 0, stop=k == KD - 1)
                    m.then_inc(done, 1)

            def down(it, s):
                t, p, u = it * spi + s, s % 2, s // spb
                pe.wait_ge(s_alo, t + 1)
                pe.wait_ge(s_dlo, t + 1)
                first, last = s % spb == 0, s % spb == spb - 1
                if first:
                    wait(pe, s_acc, BLK * (it * 2 + u - 1))
                for c in range(2):
                    for k in range(KD):
                        q = GU + c * D + k * P
                        m = split3(mm, ps_out[u][:, k * BT:(k + 1) * BT], whl[:, p, 0, q:q + P],
                                   whl[:, p, 1, q:q + P], ahl[:, p, 0, c * BT:(c + 1) * BT],
                                   ahl[:, p, 1, c * BT:(c + 1) * BT], start=first and c == 0 and k == 0,
                                   stop=last and c == 1, skip_group_check=True)
                m.then_inc(s_dn, 1)

            def body(it, last):
                for s in range(spi):
                    project(it, s)
                    if s > 0:
                        down(it, s - 1)
                    elif not (isinstance(it, int) and it == 0):
                        down(it - 1, spi - 1)
                if last:
                    down(it, spi - 1)

            rounds(pe, n_it, body)

        @block.scalar
        def _(se):
            if layer == 2:
                resplit_hi(nc, se, mem, s_xhi)

            def split_gu(it, s):
                t, p = it * spi + s, s % 2
                se.wait_ge(s_raw[s % RAWS], per_load * turns(it, s))
                wait(se, s_up, t - 1)
                se.activation(whl[:, p, 0, 0:GU], raw[:, s % RAWS, 0:GU], ACT.Copy).then_inc(s_whi, 1)

            def split_dn(it, s):
                t, p = it * spi + s, s % 2
                wait(se, s_dn, t - 1)
                se.activation(whl[:, p, 0, GU:], raw[:, s % RAWS, GU:], ACT.Copy).then_inc(s_dhi, 1)

            split_gu(0, 0)
            split_gu(0, 1)
            split_dn(0, 0)
            expert = [None]

            def body(it, last):
                for s in range(spi):
                    t, p = it * spi + s, s % 2
                    if layer == 2 and s % spb == 0:
                        expert[0] = se.value_load(eblk[0:1, ds(it * 2 + s // spb, 1)],
                                                  min_val=0, max_val=NE - 1)
                    se.wait_ge(s_gate, t + 1)
                    if layer == 1:
                        se.activation(gel[:, p, :], ps_gate[p][:, :], ACT.Gelu_apprx_tanh).then_inc(s_gel, 1)
                    else:
                        for c in range(2):
                            m = se.activation(gel[:, p, c * BT:(c + 1) * BT], ps_gate[p][:, c * BT:(c + 1) * BT],
                                              ACT.Silu, bias=btab[:, ds(expert[0] * 4 + (s % spb) * 2 + c, 1)])
                        m.then_inc(s_gel, 1)
                    if not (last and s + 2 >= spi):
                        split_gu(it + (s + 2) // spi, (s + 2) % spi)
                    se.wait_ge(s_act, t + 1)
                    wait(se, s_dn, t - 1)
                    se.activation(ahl[:, p, 0, :], act[:, p, :], ACT.Copy).then_inc(s_ahi, 1)
                    if not (last and s + 1 >= spi):
                        split_dn(it + (s + 1) // spi, (s + 1) % spi)

            rounds(se, n_it, body)

        @block.vector
        def _(dve):
            if layer == 2:
                resplit_lo(nc, dve, mem, s_xhi, s_xlo)
                dve.wait_ge(s_xlo, RESPLIT)
                n = NB // RESPLIT
                for c in range(RESPLIT):
                    a = acc[:, c * n:(c + 1) * n, :, :].rearrange("p b k t -> p (b k) t")
                    bias = mem["bdn_b"][:, c * n:(c + 1) * n, :].rearrange("p b k -> p (b k)")
                    nc.vector.tensor_tensor(a, a, bias.unsqueeze(2).broadcast_to([P, n * KD, TOK]),
                                            ALU.add).then_inc(s_xlo, 1)
                dve.wait_ge(s_xlo, 2 * RESPLIT)

            def split_gu(it, s):
                t, p = it * spi + s, s % 2
                dve.wait_ge(s_whi, t + 1)
                nc.vector.tensor_tensor(whl[:, p, 1, 0:GU], raw[:, s % RAWS, 0:GU],
                                        whl[:, p, 0, 0:GU].bitcast(F32), ALU.subtract).then_inc(s_wlo, 1)

            def split_dn(it, s):
                t, p = it * spi + s, s % 2
                dve.wait_ge(s_dhi, t + 1)
                nc.vector.tensor_tensor(whl[:, p, 1, GU:], raw[:, s % RAWS, GU:],
                                        whl[:, p, 0, GU:].bitcast(F32), ALU.subtract).then_inc(s_dlo, 1)

            def add(it, u, is_shared):
                b = it * 2 + u
                dve.wait_ge(s_dn, spb * (b + 1))
                if is_shared:
                    a = acc[:, ds(b * BLK, BLK), :, :]
                    nc.vector.tensor_tensor(
                        a, a, ps_out[u][:, :].rearrange("p (k b t) -> p b k t", k=KD, b=BLK),
                        ALU.add).then_inc(s_acc, BLK)
                    return
                slot0 = (b - 2 * n_sh) * BLK
                for j in range(BLK):
                    batch = dve.value_load(bslot[0:1, ds(slot0 + j, 1)], min_val=0, max_val=NB - 1)
                    a = acc[:, ds(batch, 1), :, :].rearrange("p b k t -> p (b k) t")
                    wait(dve, s_acc, BLK * b + j)
                    nc.vector.scalar_tensor_tensor(
                        a, ps_out[u][:, :].rearrange("p (k t) -> p k t", k=KD)[:, :, j * TOK:(j + 1) * TOK],
                        wslot[:, ds(slot0 + j, 1)], a, ALU.mult, ALU.add).then_inc(s_acc, 1)

            split_gu(0, 0)
            split_gu(0, 1)
            split_dn(0, 0)
            expert = [None]

            def body(it, last, prev_shared, now_shared):
                for s in range(spi):
                    t, p = it * spi + s, s % 2
                    if layer == 2 and s % spb == 0:
                        expert[0] = dve.value_load(eblk[0:1, ds(it * 2 + s // spb, 1)],
                                                   min_val=0, max_val=NE - 1)
                    dve.wait_ge(s_gel, t + 1)
                    dve.wait_ge(s_up, t + 1)
                    if layer == 1:
                        nc.vector.tensor_tensor(act[:, p, :], ps_up[p][:, :], gel[:, p, :],
                                                ALU.mult).then_inc(s_act, 1)
                    else:
                        for c in range(2):
                            bias = btab[:, ds(expert[0] * 4 + NE * 4 + (s % spb) * 2 + c, 1)]
                            m = nc.vector.scalar_tensor_tensor(
                                act[:, p, c * BT:(c + 1) * BT], ps_up[p][:, c * BT:(c + 1) * BT], bias,
                                gel[:, p, c * BT:(c + 1) * BT], ALU.add, ALU.mult)
                        m.then_inc(s_act, 1)
                    if not (last and s + 2 >= spi):
                        split_gu(it + (s + 2) // spi, (s + 2) % spi)
                    dve.wait_ge(s_ahi, t + 1)
                    nc.vector.tensor_tensor(ahl[:, p, 1, :], act[:, p, :], ahl[:, p, 0, :].bitcast(F32),
                                            ALU.subtract).then_inc(s_alo, 1)
                    if not (last and s + 1 >= spi):
                        split_dn(it + (s + 1) // spi, (s + 1) % spi)
                    if s == spb:
                        add(it, 0, now_shared)
                    elif s == 0 and not (isinstance(it, int) and it == 0):
                        add(it - 1, 1, prev_shared)
                if last:
                    add(it, 1, now_shared)

            loop(dve, body)


def layer3(nc, sem, mem, banks, out_tok):
    xg, acc, xhl, w3hl, act, gel = (mem[k] for k in ("xg", "acc", "xhl", "w3hl", "act", "gel"))
    ident, ytab, bias3_b = mem["ident"], mem["ytab"], mem["bias3_b"]
    ps_x, ps_g = banks[0:2], banks[2:6]
    NQ = NE // 2

    s_xhi = sem("s_xhi_3")
    s_xlo = sem("s_xlo_3")
    s_st = sem("s_st")
    s_xs = sem("s_xs")
    s_xt = sem("s_xt3")
    s_g = sem("s_g")
    s_o = sem("s_o")
    s_mix = sem("s_mix")
    s_out = [sem(f"s_out_{u}") for u in range(2)]

    with nc.Block() as block:
        @block.gpsimd
        def _(pool):
            pool.wait_ge(s_xlo, RESPLIT)

            def pair(i, last):
                for u in range(2):
                    t = 2 * i + u
                    wait(pool, s_g, NQ * (t - 1))
                    pool.tensor_copy(xg[:, u, :, 0:P].rearrange("p k (b t) -> p k b t", b=2),
                                     xhl[:, ds(t * 2, 2), :, :].rearrange("p b k t -> p k b t"))\
                        .then_inc(s_st, 1)

            rounds(pool, N_TILE3 // 2, pair)

        @block.scalar
        def _(se):
            resplit_hi(nc, se, mem, s_xhi)

            def pair(i, last):
                for u in range(2):
                    t = 2 * i + u
                    wait(se, s_xt, t - 1)
                    se.activation(act[:, u, 0:D].rearrange("p (k b t) -> p k b t", k=KD, b=2),
                                  acc[:, ds(t * 2, 2), :, :].rearrange("p b k t -> p k b t"),
                                  ACT.Copy).then_inc(s_xs, 1)

            rounds(se, N_TILE3 // 2, pair)

        @block.tensor
        def _(pe):
            mm = nc.tensor.matmul

            def pair(i, last):
                for u in range(2):
                    t = 2 * i + u
                    pe.wait_ge(s_xs, t + 1)
                    wait(pe, s_o, t - 1)
                    for k in range(KD):
                        m = nc.tensor.transpose(ps_x[u][:, k * P:(k + 1) * P], act[:, u, k * P:(k + 1) * P],
                                                ident[:, :])
                    m.then_inc(s_xt, 1)
                    pe.wait_ge(s_st, t + 1)
                    for q in range(NQ):
                        wait(pe, s_mix, NE * (t - 1) + 2 * q + 2)
                        for k in range(KD):
                            w = [w3hl[:, hl, k, 2 * q:2 * q + 2, :].rearrange("p g o -> p (g o)")
                                 for hl in range(2)]
                            m = split3(mm, ps_g[q][:, :], xg[:, u, k, 0:P], xg[:, u, KD + k, 0:P],
                                       w[0], w[1], start=k == 0, stop=k == KD - 1)
                        m.then_inc(s_g, 1)

            rounds(pe, N_TILE3 // 2, pair)

        @block.vector
        def _(dve):
            resplit_lo(nc, dve, mem, s_xhi, s_xlo)

            def pair(i, last):
                for u in range(2):
                    t = 2 * i + u
                    o = gel[:, u, 0:D]
                    dve.wait_ge(s_xt, t + 1)
                    wait(dve, s_out[u], 16 * i)
                    nc.vector.tensor_tensor(o, ps_x[u][:, 0:D], bias3_b[:, :], ALU.add).then_inc(s_o, 1)
                    dve.wait_ge(s_o, t + 1)
                    for g in range(NE):
                        dve.wait_ge(s_g, NQ * t + g // 2 + 1)
                        wait(dve, s_mix, NE * t + g)
                        nc.vector.scalar_tensor_tensor(
                            o, ps_g[g // 2][:, (g % 2) * D:(g % 2 + 1) * D],
                            ytab[:, ds(t, 1), g:g + 1].rearrange("p a b -> p (a b)"), o,
                            ALU.mult, ALU.add).then_inc(s_mix, 1)

            rounds(dve, N_TILE3 // 2, pair)

        @block.sync
        def _(sp):
            def pair(i, last):
                for u in range(2):
                    t = 2 * i + u
                    sp.wait_ge(s_mix, NE * (t + 1))
                    sp.dma_start(out_tok[ds(t * P, P), :], gel[:, u, 0:D]).then_inc(s_out[u], 16)

            rounds(sp, N_TILE3 // 2, pair)
            for u in range(2):
                sp.wait_ge(s_out[u], 16 * (N_TILE3 // 2))


_INS = ["x", "cond_8", "L0_cond_W_base", "L0_cond_b_base", "L0_cond_As", "L0_cond_Bs",
        "L1_cond_skill_gate", "L1_cond_skill_up", "L1_cond_skill_down",
        "L1_cond_shared_gate", "L1_cond_shared_up", "L1_cond_shared_down",
        "L2_cond_W_up", "L2_cond_b_up", "L2_cond_W_gate", "L2_cond_b_gate", "L2_cond_W_down",
        "L2_cond_b_down", "L3_cond_weight", "L3_cond_mask", "L3_cond_bias"]


def kernel(**inputs):
    import concourse.bacc as bacc
    from concourse.bass_utils import run_bass_kernel_spmd

    nc = bacc.Bacc("TRN2", target_bir_lowering=False, num_devices=1)
    arrays, args = {}, []
    for name in _INS:
        a = np.ascontiguousarray(inputs[name])
        arrays[f"in_{name}"] = a
        args.append(nc.dram_tensor(f"in_{name}", a.shape, mybir.dt.from_np(a.dtype), kind="ExternalInput").ap())
    args.append(nc.dram_tensor("out_0", (NB, TOK, D), F32, kind="ExternalOutput").ap())
    build(nc, *args)
    r = run_bass_kernel_spmd(nc, [arrays], core_ids=[0])
    return r.results[0]["out_0"]
```

```python
from contextlib import ExitStack

import numpy as np

import concourse.bass as bass
from concourse import mybir

ALU = mybir.AluOpType
ACT = mybir.ActivationFunctionType
AX_X = mybir.AxisListType.X
F32 = mybir.dt.float32
F32R = mybir.dt.float32r
BF16 = mybir.dt.bfloat16
I32 = mybir.dt.int32
U32 = mybir.dt.uint32
ds = bass.ds

P = 128
NB, TOK, D = 64, 64, 256
NE = 8
KD = D // P
BLK = 4
BT = BLK * TOK
CH = 2 * BT
I1 = 1024
H2 = 512
STEPH = 256
WCOL = 3 * CH
RAWS = 4
N_SHARED = NB // BLK
N_TOP2 = (2 * NB + NE * (BLK - 1)) // BLK
N_TOP1 = (NB + NE * (BLK - 1)) // BLK
SLOTS1, SLOTS2 = N_TOP2 * BLK, N_TOP1 * BLK
assert N_SHARED % 2 == 0 and N_TOP2 % 2 == 0 and N_TOP1 % 2 == 0
assert I1 == 4 * STEPH and H2 == 2 * STEPH
R_LORA = 16
SCALING = 2.0
N_TILE0 = NB // BLK
GB = 16
NG = NB // GB
SL = 4
PARTS = 3
EYE = PARTS * SL * NE
ROWS3 = EYE + SL
COL3 = KD * D // SL * P
STAGE = 512
N_STAGE = COL3 // STAGE
PIECE_STEPS = 6


def wait(eng, sem, value):
    if not isinstance(value, int) or value > 0:
        eng.wait_ge(sem, value)


def rounds(eng, n, body):
    body(0, False)
    with eng.Fori(1, n - 1) as i:
        body(i, False)
    body(n - 1, True)


def build(nc, d):
    with ExitStack() as whole:
        def sem(name):
            return whole.enter_context(nc.semaphore(name))

        def into(stack):
            return lambda name, shape, dt=F32: stack.enter_context(nc.sbuf_tensor(name, shape, dt))

        sb = into(whole)
        mem = dict(
            acc=sb("acc", [P, NB, KD, TOK]),
            xg=sb("xg", [P, 2, 2 * KD, BT], F32R),
            gel=sb("gel", [P, 2, CH]),
            parts=sb("parts", [P, COL3], BF16),
            ysel=sb("ysel", [P, PARTS, NG, SL, GB], BF16),
        )
        banks = [whole.enter_context(nc.psum_tensor(f"bank{i}", [P, CH], F32)) for i in range(8)]
        s_raw = {layer: [sem(f"s_raw{r}_{layer}") for r in range(RAWS)] for layer in (1, 2)}

        with ExitStack() as phase:
            sb = into(phase)
            stage = sb("stage", [P, 2, STAGE])
            mem.update(
                xhl=sb("xhl", [P, NB, 2 * KD, TOK], F32R),
                raw=sb("raw", [P, RAWS, WCOL]),
                whl=sb("whl", [P, 2, 2, WCOL], F32R),
                act=sb("act", [P, 2, CH]),
                ahl=sb("ahl", [P, 2, 2, CH], F32R),
                stage=stage,
                zero=sb("zero", [P, 1]),
                piece=stage[:, 1, 0:STAGE // 2].bitcast(BF16),
                btab=stage[:, 1, 0:2 * NE * 4],
                bdn_b=stage[:, 0, 0:NB * KD].rearrange("p (b k) -> p b k", k=KD),
                wslot1=sb("wslot1", [P, SLOTS1]),
                wslot2=sb("wslot2", [P, SLOTS2]),
                bslot1=sb("bslot1", [1, SLOTS1], I32),
                bslot2=sb("bslot2", [1, SLOTS2], I32),
                eblk1=sb("eblk1", [1, N_TOP2], I32),
                eblk2=sb("eblk2", [1, N_TOP1], I32),
            )
            layer0(nc, sem, mem, banks, d, s_raw)
            mlp(nc, sem, mem, banks, d, 1, s_raw)
            mlp(nc, sem, mem, banks, d, 2, s_raw)

        with ExitStack() as phase:
            sb = into(phase)
            mem.update(
                wbot=sb("wbot", [P, 2, GB, 2, KD * D], F32R),
                bias3_b=sb("bias3_b", [P, D]),
            )
            layer3(nc, sem, mem, banks, d["bias3"], d["out"])


def load_step(sp, mem, wts, s_raw, expert, q, slot):
    sp.dma_start(mem["raw"][:, slot, :], wts[ds(expert, 1), q].rearrange("e p w -> p (e w)"))\
        .then_inc(s_raw[slot], 16)


def layer0(nc, sem, mem, banks, d, s_raw):
    xg, ahl, acc, xhl, whl, ysel = (mem[k] for k in ("xg", "ahl", "acc", "xhl", "whl", "ysel"))
    W_OFF, A_OFF, B_OFF = 0, CH, CH + D
    hs = [mem["act"][:, 1, u * BT:(u + 1) * BT] for u in range(2)]
    x0hl = [xg[:, u, :, :] for u in range(2)]
    hshl = [ahl[:, u, :, 0:BT] for u in range(2)]
    ps_h, ps_y, b7 = banks[0:2], banks[2:4], banks[7]
    w0 = mem["gel"][:, :, :].rearrange("p u w -> p (u w)")
    work = mem["raw"][:, :, :].rearrange("p s w -> p (s w)")
    at = [0]

    def rb(parts, *shape, dt=F32):
        n = int(np.prod(shape))
        view = work[0:parts, at[0]:at[0] + n]
        at[0] += n
        assert at[0] <= RAWS * WCOL
        if dt is not F32:
            view = view.bitcast(dt)
        if len(shape) == 2:
            view = view.rearrange("p (a b) -> p a b", a=shape[0])
        if len(shape) == 3:
            view = view.rearrange("p (a b c) -> p a b c", a=shape[0], b=shape[1])
        return view

    cnd = rb(NB, NE)
    ident = rb(P, P)
    bias0 = rb(P, KD)
    wexp = rb(P, NB)
    top = rb(NB, 8)
    topi = rb(NB, 8, dt=U32)
    topf = rb(NB, 8)
    ntop = rb(NB, 1)
    ex = rb(NB, 8)
    prob = rb(NB, 12)
    hot = rb(NB, 3, NE)
    iota_e = rb(NB, NE)
    tri = rb(NB, NB)
    ones = rb(NB, P)
    iota_b = rb(NB, P)
    iota_s = rb(NB, SLOTS1)
    icnt = rb(P, 2, NE, dt=I32)
    run = rb(P, 3, 2, NE)
    first = rb(P, 2, NE)
    rank = rb(NB, 2, NE)
    pos = rb(NB, 2, NE)
    hpos = rb(NB, 3, NE)
    onehot = rb(NB, 2 * SLOTS1 + SLOTS2)
    wb = rb(NB, 2, P)
    hotT = rb(NE, NB)
    bdn_n = rb(NE, D)
    iota4 = rb(1, N_TOP2)
    ended = rb(1, N_TOP2, NE)
    n_ended = rb(1, N_TOP2)
    yrep = rb(P, NB)
    ypart = rb(P, NB // 2).bitcast(BF16)
    delta = rb(P, SL)

    s_const = sem("s_const")
    s_cond = sem("s_cond")
    s_small = sem("s_small")
    s_w0 = sem("s_w0")
    s_route = sem("s_route")
    s_table = sem("s_table")
    s_exp = sem("s_exp")
    s_sel = sem("s_sel")
    s_w0hi = sem("s_w0hi")
    s_w0lo = sem("s_w0lo")
    s_x = sem("s_x")
    s_x0hi = sem("s_x0hi")
    s_x0lo = sem("s_x0lo")
    s_h = sem("s_h")
    s_hs = sem("s_hs")
    s_hshi = sem("s_hshi")
    s_hslo = sem("s_hslo")
    s_y = sem("s_y")
    s_x1 = sem("s_x1")
    s_x1hi = sem("s_x1hi")
    s_x1lo = sem("s_x1lo")
    s_ysel = sem("s_ysel")
    s_done = sem("s_done")
    mark = {}

    with nc.Block() as block:
        @block.sync
        def _(sp):
            sp.dma_start(cnd, d["cond"]).then_inc(s_cond, 16)
            sp.dma_start(w0, d["w0"]).then_inc(s_w0, 16)
            def load_x(i):
                wait(sp, s_x, 16 * i)
                sp.dma_start(acc[:, ds(2 * BLK * i, 2 * BLK), :, :].rearrange("p b k t -> p (b k t)"),
                             d["x"][:, ds(2 * BLK * i, 2 * BLK), :, :].rearrange("p b k t -> p (b k t)"))\
                    .then_inc(s_x, 16)

            load_x(0)
            small = ((bias0, d["bias0"]), (wexp, d["wexp"]), (bdn_n, d["bdown2"]),
                     (yrep, d["yrep"]), (delta, d["delta"]))
            for dst, src in small:
                sp.dma_start(dst, src).then_inc(s_small, 16)
            mark["small"] = 16 * len(small)
            with sp.Fori(1, N_TILE0 // 2) as i:
                load_x(i)

            sp.wait_ge(s_done, 1)
            for r in range(RAWS):
                load_step(sp, mem, d["w1"], s_raw[1], NE, r, r)

        @block.gpsimd
        def _(pool):
            pool.memset(ident, 0.0).then_inc(s_const, 1)
            pool.memset(tri, 0.0).then_inc(s_const, 1)
            pool.memset(ones, 1.0).then_inc(s_const, 1)
            pool.memset(mem["zero"][:, :], 0.0)
            for dst, pattern, channel in ((iota_e, [[1, NE]], 0), (iota_b, [[0, P]], 1),
                                          (iota_s, [[1, SLOTS1]], 0), (iota4, [[BLK, N_TOP2]], 0)):
                pool.iota(dst, pattern, base=0, channel_multiplier=channel,
                          allow_small_or_imprecise_dtypes=True).then_inc(s_const, 1)
            pool.wait_ge(s_const, 7)
            pool.affine_select(out=ident, in_=ident, compare_op=ALU.not_equal, fill=1.0,
                               base=0, pattern=[[-1, P]], channel_multiplier=1).then_inc(s_const, 1)
            pool.affine_select(out=tri, in_=tri, compare_op=ALU.is_ge, fill=1.0,
                               base=0, pattern=[[-1, NB]], channel_multiplier=1).then_inc(s_const, 1)

            steps = [0]

            def step(ins):
                steps[0] += 1
                ins.then_inc(s_table, 1)
                pool.wait_ge(s_table, steps[0])

            pool.wait_ge(s_route, ROUTED)
            for shift, a, b in ((1, 0, 1), (2, 1, 2), (4, 2, 1)):
                step(pool.tensor_copy(run[:, b, :, 0:shift], run[:, a, :, 0:shift]))
                step(pool.tensor_tensor(run[:, b, :, shift:], run[:, a, :, shift:],
                                        run[:, a, :, :NE - shift], ALU.add))
            end = run[:, 1]
            step(pool.tensor_tensor(first, end, run[:, 0], ALU.subtract))
            step(pool.tensor_tensor(pos, rank, first[:NB], ALU.add))
            for k in range(2):
                step(pool.tensor_tensor(hpos[:, k, :], hot[:, k, :], pos[:, 0, :], ALU.mult))
            step(pool.tensor_tensor(hpos[:, 2, :], hot[:, 0, :], pos[:, 1, :], ALU.mult))
            for n in (4, 2, 1):
                step(pool.tensor_tensor(hpos[:, :, 0:n], hpos[:, :, 0:n], hpos[:, :, n:2 * n], ALU.add))
            assert steps[0] == N_TABLE

            steps[0] = 0

            def ystep(ins):
                steps[0] += 1
                ins.then_inc(s_ysel, 1)
                pool.wait_ge(s_ysel, steps[0])

            pool.wait_ge(s_small, mark["small"])
            ystep(pool.memset(ysel[:, :, :, :, :], 0.0))
            lead = (PARTS - 1) * SL * NE
            for v, rows in ((0, slice(0, P)), (1, slice(0, EYE)), (2, slice(lead, EYE))):
                n = rows.stop - rows.start
                for s in range(SL):
                    ystep(pool.tensor_tensor(
                        ysel[rows, v, :, s, :], yrep[rows].rearrange("p (g b) -> p g b", g=NG),
                        delta[rows, s:s + 1].unsqueeze(2).broadcast_to([n, NG, GB]), ALU.mult))
                if v < 2:
                    ystep(pool.tensor_copy(ypart, yrep))
                    ystep(pool.tensor_tensor(yrep, yrep, ypart, ALU.subtract))
            ystep(pool.memset(ysel[0:SL * NE, 1, :, :, :], 0.0))

            def split_out(t):
                pool.wait_ge(s_x1hi, t + 1)
                pool.tensor_tensor(xhl[:, ds(t * BLK, BLK), KD:, :], acc[:, ds(t * BLK, BLK), :, :],
                                   xhl[:, ds(t * BLK, BLK), 0:KD, :].bitcast(F32),
                                   ALU.subtract).then_inc(s_x1lo, 1)

            with pool.Fori(0, N_TILE0) as t:
                split_out(t)

        @block.vector
        def _(dve):
            steps = [0]

            def step(ins):
                steps[0] += 1
                ins.then_inc(s_route, 1)
                dve.wait_ge(s_route, steps[0])

            dve.wait_ge(s_cond, 16)
            step(nc.vector.max(top, cnd))
            step(nc.vector.tensor_scalar(ntop, top[:, 0:1], -1.0, None, ALU.mult))
            step(nc.vector.max_index(topi, top, cnd))
            step(nc.vector.tensor_copy(topf, topi))
            dve.wait_ge(s_const, 9)
            for k in range(2):
                step(nc.vector.tensor_scalar(hot[:, k, :], iota_e, topf[:, k:k + 1], None, ALU.is_equal))
            step(nc.vector.tensor_tensor(hot[:, 2, :], hot[:, 0, :], hot[:, 1, :], ALU.add))
            mark["hot"] = steps[0]
            dve.wait_ge(s_exp, 1)
            step(nc.vector.reduce_sum(prob[:, 0:1], ex, AX_X))
            step(nc.vector.reciprocal(prob[:, 1:2], prob[:, 0:1]))
            step(nc.vector.tensor_scalar(prob[:, 2:4], ex[:, 0:2], prob[:, 1:2], None, ALU.mult))
            step(nc.vector.tensor_tensor(prob[:, 4:5], prob[:, 2:3], prob[:, 3:4], ALU.add))
            step(nc.vector.reciprocal(prob[:, 5:6], prob[:, 4:5]))
            step(nc.vector.tensor_scalar(prob[:, 6:8], prob[:, 2:4], prob[:, 5:6], None, ALU.mult))
            step(nc.vector.tensor_scalar(prob[:, 8:10], prob[:, 6:8], 1.0 - 1.0 / 12, None, ALU.mult))
            step(nc.vector.scalar_tensor_tensor(prob[:, 10:12], prob[:, 6:8], 1.0 / 12, prob[:, 8:10],
                                                ALU.mult, ALU.add))
            for k in range(2):
                step(nc.vector.tensor_scalar(wb[:, k, :], ones, prob[:, 10 + k:11 + k], None, ALU.mult))
            dve.wait_ge(s_sel, 1)
            step(nc.vector.tensor_scalar(icnt, b7[:, 16:32].rearrange("p (a e) -> p a e", a=2),
                                         float(BLK - 1), None, ALU.add))
            step(nc.vector.tensor_scalar(icnt, icnt, BLK.bit_length() - 1, BLK.bit_length() - 1,
                                         ALU.logical_shift_right, ALU.logical_shift_left))
            step(nc.vector.tensor_copy(run[:, 0], icnt))
            step(nc.vector.tensor_copy(rank, b7[:NB, 0:16].rearrange("p (a e) -> p a e", a=2)))
            step(nc.vector.tensor_copy(hotT, b7[:NE, 64:64 + NB]))
            assert steps[0] == ROUTED
            dve.wait_ge(s_small, mark["small"])
            step(nc.vector.tensor_scalar(wexp, wexp, SCALING, None, ALU.mult))

            for b in range(2):
                dve.wait_ge(s_w0hi, b + 1)
                nc.vector.tensor_tensor(whl[:, 0, 1, b * CH:(b + 1) * CH], w0[:, b * CH:(b + 1) * CH],
                                        whl[:, 0, 0, b * CH:(b + 1) * CH].bitcast(F32),
                                        ALU.subtract).then_inc(s_w0lo, 1)

            def tile_in(t, u):
                dve.wait_ge(s_x0hi, t + 1)
                x0 = acc[:, ds(t * BLK, BLK), :, :].rearrange("p b k t -> p k b t")
                nc.vector.tensor_tensor(x0hl[u][:, KD:, :].rearrange("p k (b t) -> p k b t", b=BLK), x0,
                                        x0hl[u][:, 0:KD, :].rearrange("p k (b t) -> p k b t", b=BLK)
                                        .bitcast(F32), ALU.subtract).then_inc(s_x0lo, 1)

            tile_in(0, 0)

            def sum_out(t, u):
                dve.wait_ge(s_y, t + 1)
                for c in range(KD):
                    a = acc[:, ds(t * BLK, BLK), c, :]
                    m = nc.vector.scalar_tensor_tensor(
                        a, ps_y[u][:, c * BT:(c + 1) * BT].rearrange("p (b t) -> p b t", b=BLK),
                        bias0[:, c:c + 1], a, ALU.add, ALU.add)
                m.then_inc(s_x1, 1)

            def pair(i, last):
                for u in range(2):
                    t = 2 * i + u
                    inner = not (isinstance(t, int) and t == 0)
                    dve.wait_ge(s_h, t + 1)
                    w = wexp[:, ds(t * BLK, BLK)].unsqueeze(2).broadcast_to([P, BLK, TOK])
                    nc.vector.tensor_tensor(hs[u].rearrange("p (b t) -> p b t", b=BLK),
                                            ps_h[u][:, 0:BT].rearrange("p (b t) -> p b t", b=BLK), w,
                                            ALU.mult).then_inc(s_hs, 1)
                    if inner:
                        sum_out(t - 1, 1 - u)
                    dve.wait_ge(s_hshi, t + 1)
                    nc.vector.tensor_tensor(hshl[u][:, 1, :], hs[u], hshl[u][:, 0, :].bitcast(F32),
                                            ALU.subtract).then_inc(s_hslo, 1)
                    if not (last and u == 1):
                        tile_in(t + 1, 1 - u)
                if last:
                    sum_out(t, 1)

            rounds(dve, N_TILE0 // 2, pair)
            dve.wait_ge(s_table, N_TABLE)
            for k in range(3):
                width = SLOTS1 if k < 2 else SLOTS2
                step(nc.vector.tensor_scalar(onehot[:, k * SLOTS1:k * SLOTS1 + width], iota_s[:, :width],
                                             hpos[:, k, 0:1], None, ALU.is_equal))
            mark["onehot"] = steps[0]
            for a, n, tab in ((0, N_TOP2, "eblk1"), (1, N_TOP1, "eblk2")):
                step(nc.vector.tensor_tensor(ended[:, :n, :], iota4[:, :n].unsqueeze(2).broadcast_to([1, n, NE]),
                                             run[0:1, 1, a, :].unsqueeze(1).broadcast_to([1, n, NE]),
                                             ALU.is_ge))
                step(nc.vector.reduce_sum(n_ended[:, :n], ended[:, :n, :], AX_X))
                step(nc.vector.tensor_scalar(mem[tab][:, :], n_ended[:, :n], float(NE - 1), None, ALU.min))
            dve.wait_ge(s_sel, 3)
            step(nc.vector.tensor_copy(mem["wslot1"][:, :], b7[:, 0:SLOTS1]))
            step(nc.vector.tensor_copy(mem["bslot1"][:, :], b7[0:1, 160:160 + SLOTS1]))
            step(nc.vector.tensor_copy(mem["wslot2"][:, :], b7[:, 320:320 + SLOTS2]))
            step(nc.vector.tensor_copy(mem["bslot2"][:, :], b7[0:1, 416:416 + SLOTS2]))
            dve.wait_ge(s_ysel, N_YSEL)
            nc.vector.tensor_copy(ident[0:1, 0:1], ident[0:1, 0:1]).then_inc(s_done, 1)

        @block.scalar
        def _(se):
            se.wait_ge(s_route, 2)
            se.activation(ex, top, ACT.Exp, bias=ntop[:, 0:1]).then_inc(s_exp, 1)
            se.wait_ge(s_w0, 16)
            for b in range(2):
                se.activation(whl[:, 0, 0, b * CH:(b + 1) * CH], w0[:, b * CH:(b + 1) * CH],
                              ACT.Copy).then_inc(s_w0hi, 1)

            def tile_in(t, u, n):
                se.wait_ge(s_x, 16 * n)
                wait(se, s_y, t - 1)
                se.activation(x0hl[u][:, 0:KD, :].rearrange("p k (b t) -> p k b t", b=BLK),
                              acc[:, ds(t * BLK, BLK), :, :].rearrange("p b k t -> p k b t"),
                              ACT.Copy).then_inc(s_x0hi, 1)

            tile_in(0, 0, 1)

            def tile_out(t, u):
                se.wait_ge(s_x1, t + 1)
                se.activation(xhl[:, ds(t * BLK, BLK), 0:KD, :], acc[:, ds(t * BLK, BLK), :, :],
                              ACT.Copy).then_inc(s_x1hi, 1)

            def pair(i, last):
                for u in range(2):
                    t = 2 * i + u
                    se.wait_ge(s_hs, t + 1)
                    wait(se, s_y, t - 1)
                    se.activation(hshl[u][:, 0, :], hs[u], ACT.Copy).then_inc(s_hshi, 1)
                    if not (last and u == 1):
                        tile_in(t + 1, 1 - u, i + 1 + u)
                    if not (isinstance(t, int) and t == 0):
                        tile_out(t - 1, 1 - u)
                if last:
                    tile_out(t, 1)

            rounds(se, N_TILE0 // 2, pair)

        @block.tensor
        def _(pe):
            mm = nc.tensor.matmul
            pe.wait_ge(s_const, 9)
            pe.wait_ge(s_route, mark["hot"])
            mm(b7[:NB, 0:8], tri, hot[:, 2, :], start=True, stop=True)
            mm(b7[:NB, 8:16], tri, hot[:, 0, :], start=True, stop=True)
            mm(b7[:, 16:24], ones, hot[:, 2, :], start=True, stop=True)
            mm(b7[:, 24:32], ones, hot[:, 0, :], start=True, stop=True)
            mm(b7[:NE, 64:64 + NB], hot[:, 0, :], ident[:NB, :NB], start=True, stop=True).then_inc(s_sel, 1)
            pe.wait_ge(s_route, ROUTED)
            pe.wait_ge(s_small, mark["small"])
            for k in range(KD):
                last = mm(banks[6][:, k * NB:(k + 1) * NB], bdn_n[:, k * P:(k + 1) * P], hotT,
                          start=True, stop=True)
            last.then_inc(s_sel, 1)

            def w(hl, o):
                return whl[:, 0, hl, o:o + P]

            pe.wait_ge(s_w0lo, 2)

            def pair(i, last):
                for u in range(2):
                    t = 2 * i + u
                    pe.wait_ge(s_x0lo, t + 1)
                    wait(pe, s_hs, t - 1)
                    for k in range(KD):
                        o = A_OFF + k * P
                        m = split3(mm, ps_h[u][:, 0:BT], w(0, o), w(1, o), x0hl[u][:, k, :], x0hl[u][:, KD + k, :],
                                   start=k == 0, stop=k == KD - 1)
                    m.then_inc(s_h, 1)
                    wait(pe, s_x1, t - 1)
                    for c in range(KD):
                        for k in range(KD):
                            o = W_OFF + k * D + c * P
                            split3(mm, ps_y[u][:, c * BT:(c + 1) * BT], w(0, o), w(1, o), x0hl[u][:, k, :],
                                   x0hl[u][:, KD + k, :], start=c == 0 and k == 0, stop=False,
                                   skip_group_check=True)
                    pe.wait_ge(s_hslo, t + 1)
                    for c in range(KD):
                        o = B_OFF + c * P
                        m = split3(mm, ps_y[u][:, c * BT:(c + 1) * BT], w(0, o), w(1, o), hshl[u][:, 0, :],
                                   hshl[u][:, 1, :], start=False, stop=True, skip_group_check=True)
                    m.then_inc(s_y, 1)

            rounds(pe, N_TILE0 // 2, pair)
            pe.wait_ge(s_route, mark["onehot"])
            for lhs, o in (((wb[:, 0, :], wb[:, 1, :]), 0), ((iota_b, iota_b), 160)):
                for k in range(2):
                    mm(b7[:, o:o + SLOTS1], lhs[k], onehot[:, k * SLOTS1:(k + 1) * SLOTS1],
                       start=k == 0, stop=k == 1)
            for lhs, o in ((ones, 320), (iota_b, 416)):
                last = mm(b7[:, o:o + SLOTS2], lhs, onehot[:, 2 * SLOTS1:], start=True, stop=True)
            last.then_inc(s_sel, 1)


ROUTED = 22
N_TABLE = 14
N_YSEL = 2 + PARTS * SL + 4


def split3(mm, out, w_hi, w_lo, x_hi, x_lo, start, stop, **kw):
    mm(out, w_lo, x_hi, start=start, stop=False, **kw)
    mm(out, w_hi, x_lo, start=False, stop=False, **kw)
    return mm(out, w_hi, x_hi, start=False, stop=stop, **kw)


RESPLIT = 8
BY_POOL = 2


def resplit_hi(nc, se, mem, s_hi):
    n = NB // RESPLIT
    for c in range(RESPLIT):
        se.activation(mem["xhl"][:, c * n:(c + 1) * n, 0:KD, :], mem["acc"][:, c * n:(c + 1) * n, :, :],
                      ACT.Copy).then_inc(s_hi, 1)


def resplit_lo(eng, mem, s_hi, s_lo, pieces):
    n = NB // RESPLIT
    for c in pieces:
        eng.wait_ge(s_hi, c + 1)
        eng.tensor_tensor(mem["xhl"][:, c * n:(c + 1) * n, KD:, :], mem["acc"][:, c * n:(c + 1) * n, :, :],
                          mem["xhl"][:, c * n:(c + 1) * n, 0:KD, :].bitcast(F32),
                          ALU.subtract).then_inc(s_lo, 1)


POOL_PIECES = range(BY_POOL)
DVE_PIECES = range(BY_POOL, RESPLIT)


def mlp(nc, sem, mem, banks, d, layer, s_raws):
    raw, whl, xg, gel, act, ahl = (mem[k] for k in ("raw", "whl", "xg", "gel", "act", "ahl"))
    acc, xhl, btab = mem["acc"], mem["xhl"], mem["btab"]
    wslot, bslot, eblk = mem[f"wslot{layer}"], mem[f"bslot{layer}"], mem[f"eblk{layer}"]
    spb = 4 if layer == 1 else 2
    spi = 2 * spb
    n_sh = N_SHARED // 2 if layer == 1 else 0
    wts, s_raw = d[f"w{layer}"], s_raws[layer]
    n_it = n_sh + (N_TOP2 if layer == 1 else N_TOP1) // 2
    ps_gate, ps_up, ps_out = banks[0:2], banks[2:4], banks[4:6]
    act1, y = act[:, 0, :], act[:, 1, :]
    GU = 2 * CH

    L = f"_{layer}"
    s_whi = sem("s_whi" + L)
    s_wlo = sem("s_wlo" + L)
    s_dhi = sem("s_dhi" + L)
    s_dlo = sem("s_dlo" + L)
    s_xg = sem("s_xg" + L)
    s_gate = sem("s_gate" + L)
    s_up = sem("s_up" + L)
    s_gel = sem("s_gel" + L)
    s_act = sem("s_act" + L)
    s_ahi = sem("s_ahi" + L)
    s_alo = sem("s_alo" + L)
    s_dn = sem("s_dn" + L)
    s_y = sem("s_y" + L)
    s_add = sem("s_add" + L)
    s_btab = sem("s_btab" + L)
    s_bdn = sem("s_bdn" + L)
    s_bias = sem("s_bias" + L)
    s_stage = sem("s_stage" + L)
    s_part = sem("s_part" + L)
    s_xhi = sem("s_xhi" + L)
    s_xlo = sem("s_xlo" + L)

    def loop(eng, body):
        body(0, False, bool(n_sh), bool(n_sh))
        if n_sh:
            with eng.Fori(1, n_sh) as i:
                body(i, False, True, True)
            body(n_sh, False, True, False)
        with eng.Fori(n_sh + 1, n_it - 1) as i:
            body(i, False, False, False)
        body(n_it - 1, True, False, False)

    def turns(it, s):
        return it * (spi // RAWS) + s // RAWS + 1

    pieces_shared = 2 * (n_sh - 1)
    assert layer == 2 or pieces_shared + n_it - n_sh - 1 == N_STAGE

    with nc.Block() as block:
        @block.sync
        def _(sp):
            def load_stage(c):
                wait(sp, s_part, PIECE_STEPS * c)
                for a, name in enumerate(("weight3", "mask3")):
                    sp.dma_start(mem["stage"][0:ROWS3, a, :], d[name][:, ds(c * STAGE, STAGE)])\
                        .then_inc(s_stage, 16)

            def load(it, is_shared, first=0, pieces=()):
                for s in range(first, spi):
                    if s % spb == 0 and s // spb < len(pieces):
                        load_stage(pieces[s // spb])
                    t = it * spi + s
                    if is_shared:
                        e = NE
                    elif s % spb == 0 or s == first:
                        e = sp.value_load(eblk[0:1, ds((it - n_sh) * 2 + s // spb, 1)],
                                          min_val=0, max_val=NE - 1)
                    wait(sp, s_wlo, t - RAWS + 1)
                    wait(sp, s_dlo, t - RAWS + 1)
                    load_step(sp, mem, wts, s_raw, e, s % spb, s % RAWS)

            if layer == 2:
                sp.dma_start(btab, d["btab"]).then_inc(s_btab, 16)
            if spi > RAWS:
                load(0, bool(n_sh), RAWS)
            if n_sh:
                load(1, True, pieces=(0, 1))
                with sp.Fori(2, n_sh) as i:
                    load(i, True, pieces=(2 * i - 2, 2 * i - 1))
                load(n_sh, False)
                with sp.Fori(n_sh + 1, n_it) as i:
                    load(i, False, pieces=(i - n_sh - 1 + pieces_shared,))
            else:
                with sp.Fori(1, n_it) as i:
                    load(i, False)
            if layer == 1:
                for r in range(RAWS):
                    t = n_it * spi + r
                    if r % 2 == 0:
                        e = sp.value_load(mem["eblk2"][0:1, r // 2:r // 2 + 1], min_val=0, max_val=NE - 1)
                    sp.wait_ge(s_wlo, t - RAWS + 1)
                    sp.wait_ge(s_dlo, t - RAWS + 1)
                    load_step(sp, mem, d["w2"], s_raws[2], e, r % 2, r)

        @block.gpsimd
        def _(pool):
            if layer == 2:
                resplit_lo(nc.gpsimd, mem, s_xhi, s_xlo, POOL_PIECES)
                pool.wait_ge(s_xlo, RESPLIT)

            def gather(it, u, is_shared):
                b = it * 2 + u
                wait(pool, s_up, spb * (b - 1))
                if is_shared:
                    pool.tensor_copy(xg[:, u, :, :].rearrange("p k (b t) -> p k b t", b=BLK),
                                     xhl[:, ds(b * BLK, BLK), :, :].rearrange("p b k t -> p k b t"))\
                        .then_inc(s_xg, BLK)
                    return
                for j in range(BLK):
                    batch = pool.value_load(bslot[0:1, ds((b - 2 * n_sh) * BLK + j, 1)],
                                            min_val=0, max_val=NB - 1)
                    pool.tensor_copy(xg[:, u, :, j * TOK:(j + 1) * TOK],
                                     xhl[:, ds(batch, 1), :, :].rearrange("p b k t -> p (b k) t"))\
                        .then_inc(s_xg, 1)

            def add(it, u):
                b = it * 2 + u
                slot0 = (b - 2 * n_sh) * BLK
                pool.wait_ge(s_y, b + 1)
                for j in range(BLK):
                    batch = pool.value_load(bslot[0:1, ds(slot0 + j, 1)], min_val=0, max_val=NB - 1)
                    a = acc[:, ds(batch, 1), :, :].rearrange("p b k t -> p (b k t)")
                    wait(pool, s_add, slot0 + j)
                    pool.tensor_tensor(a, a, y[:, j * KD * TOK:(j + 1) * KD * TOK], ALU.add).then_inc(s_add, 1)

            def mask_and_split(c):
                w, mask, part = mem["stage"][:, 0, :], mem["stage"][:, 1, :], mem["piece"]
                row = SL * NE

                def zero(rows):
                    return mem["zero"][0:rows, :].broadcast_to([rows, STAGE])

                pool.wait_ge(s_stage, 32 * (c + 1))
                for k, (op, args) in enumerate((
                        (pool.tensor_tensor, (w[0:ROWS3], w[0:ROWS3], mask[0:ROWS3], ALU.mult)),
                        (pool.tensor_tensor, (part[0:ROWS3], w[0:ROWS3], zero(ROWS3), ALU.add)),
                        (pool.tensor_tensor, (w[0:2 * row], w[0:2 * row], part[0:2 * row], ALU.subtract)),
                        (pool.tensor_tensor, (part[0:2 * row], w[0:2 * row], zero(2 * row), ALU.add)),
                        (pool.tensor_tensor, (part[0:row], w[0:row], part[0:row], ALU.subtract)))):
                    wait(pool, s_part, PIECE_STEPS * c + k)
                    op(*args).then_inc(s_part, 1)
                pool.wait_ge(s_part, PIECE_STEPS * c + 5)
                pool.tensor_copy(mem["parts"][0:ROWS3, ds(c * STAGE, STAGE)], part[0:ROWS3]).then_inc(s_part, 1)

            gather(0, 0, bool(n_sh))
            gather(0, 1, bool(n_sh))
            if n_sh:
                for u in range(2):
                    gather(1, u, True)
                    mask_and_split(u)
                with pool.Fori(2, n_sh) as i:
                    for u in range(2):
                        gather(i, u, True)
                        mask_and_split(2 * i - 2 + u)
                for u in range(2):
                    gather(n_sh, u, False)
            else:
                pool.wait_ge(s_bdn, 1)
                n = NB // RESPLIT
                for c in range(RESPLIT):
                    a = acc[:, c * n:(c + 1) * n, :, :].rearrange("p b k t -> p (b k) t")
                    bias = mem["bdn_b"][:, c * n:(c + 1) * n, :].rearrange("p b k -> p (b k)")
                    pool.tensor_tensor(a, a, bias.unsqueeze(2).broadcast_to([P, n * KD, TOK]),
                                       ALU.add).then_inc(s_bias, 1)
                pool.wait_ge(s_bias, RESPLIT)

            def routed(i):
                for u in range(2):
                    gather(i, u, False)
                    add(i - 1, u)
                if layer == 1:
                    mask_and_split(i - n_sh - 1 + pieces_shared)

            routed(n_sh + 1)
            with pool.Fori(n_sh + 2, n_it) as i:
                routed(i)
            for u in range(2):
                add(n_it - 1, u)

        @block.tensor
        def _(pe):
            mm = nc.tensor.matmul

            def project(it, s):
                t, p, u = it * spi + s, s % 2, s // spb
                if s % spb == 0:
                    pe.wait_ge(s_xg, BLK * (it * 2 + u + 1))
                pe.wait_ge(s_wlo, t + 1)
                for o, bank, freed, done in ((0, ps_gate[p], s_gel, s_gate), (CH, ps_up[p], s_act, s_up)):
                    wait(pe, freed, t - 1)
                    for c in range(2):
                        for k in range(KD):
                            q = o + k * STEPH + c * P
                            m = split3(mm, bank[:, c * BT:(c + 1) * BT], whl[:, p, 0, q:q + P],
                                       whl[:, p, 1, q:q + P], xg[:, u, k, :], xg[:, u, KD + k, :],
                                       start=k == 0, stop=k == KD - 1)
                    m.then_inc(done, 1)

            def down(it, s):
                t, p, u = it * spi + s, s % 2, s // spb
                pe.wait_ge(s_alo, t + 1)
                pe.wait_ge(s_dlo, t + 1)
                first, last = s % spb == 0, s % spb == spb - 1
                if first:
                    wait(pe, s_y, it * 2 + u - 1)
                for c in range(2):
                    for k in range(KD):
                        q = GU + c * D + k * P
                        m = split3(mm, ps_out[u][:, k * BT:(k + 1) * BT], whl[:, p, 0, q:q + P],
                                   whl[:, p, 1, q:q + P], ahl[:, p, 0, c * BT:(c + 1) * BT],
                                   ahl[:, p, 1, c * BT:(c + 1) * BT], start=first and c == 0 and k == 0,
                                   stop=last and c == 1, skip_group_check=True)
                m.then_inc(s_dn, 1)

            def body(it, last):
                for s in range(spi):
                    project(it, s)
                    if s > 0:
                        down(it, s - 1)
                    elif not (isinstance(it, int) and it == 0):
                        down(it - 1, spi - 1)
                if last:
                    down(it, spi - 1)

            rounds(pe, n_it, body)

        @block.scalar
        def _(se):
            def split_gu(it, s):
                t, p = it * spi + s, s % 2
                wait(se, s_up, t - 1)
                se.wait_ge(s_raw[s % RAWS], 16 * turns(it, s))
                se.activation(whl[:, p, 0, 0:GU], raw[:, s % RAWS, 0:GU], ACT.Copy).then_inc(s_whi, 1)

            def split_dn(it, s):
                t, p = it * spi + s, s % 2
                wait(se, s_dn, t - 1)
                se.activation(whl[:, p, 0, GU:], raw[:, s % RAWS, GU:], ACT.Copy).then_inc(s_dhi, 1)

            split_gu(0, 0)
            if layer == 2:
                resplit_hi(nc, se, mem, s_xhi)
                se.wait_ge(s_btab, 16)
            split_dn(0, 0)
            split_gu(0, 1)
            expert = [None]

            def body(it, last):
                for s in range(spi):
                    t, p = it * spi + s, s % 2
                    if layer == 2 and s % spb == 0:
                        expert[0] = se.value_load(eblk[0:1, ds(it * 2 + s // spb, 1)],
                                                  min_val=0, max_val=NE - 1)
                    se.wait_ge(s_gate, t + 1)
                    if layer == 1:
                        se.activation(gel[:, p, :], ps_gate[p][:, :], ACT.Gelu_apprx_tanh).then_inc(s_gel, 1)
                    else:
                        for c in range(2):
                            m = se.activation(gel[:, p, c * BT:(c + 1) * BT], ps_gate[p][:, c * BT:(c + 1) * BT],
                                              ACT.Silu, bias=btab[:, ds(expert[0] * 4 + (s % spb) * 2 + c, 1)])
                        m.then_inc(s_gel, 1)
                    if not (last and s + 2 >= spi):
                        split_gu(it + (s + 2) // spi, (s + 2) % spi)
                    se.wait_ge(s_act, t + 1)
                    wait(se, s_dn, t - 1)
                    se.activation(ahl[:, p, 0, :], act1, ACT.Copy).then_inc(s_ahi, 1)
                    if not (last and s + 1 >= spi):
                        split_dn(it + (s + 1) // spi, (s + 1) % spi)

            rounds(se, n_it, body)

        @block.vector
        def _(dve):
            def split_gu(it, s):
                t, p = it * spi + s, s % 2
                dve.wait_ge(s_whi, t + 1)
                nc.vector.tensor_tensor(whl[:, p, 1, 0:GU], raw[:, s % RAWS, 0:GU],
                                        whl[:, p, 0, 0:GU].bitcast(F32), ALU.subtract).then_inc(s_wlo, 1)

            def split_dn(it, s):
                t, p = it * spi + s, s % 2
                dve.wait_ge(s_dhi, t + 1)
                nc.vector.tensor_tensor(whl[:, p, 1, GU:], raw[:, s % RAWS, GU:],
                                        whl[:, p, 0, GU:].bitcast(F32), ALU.subtract).then_inc(s_dlo, 1)

            def output(it, u, is_shared):
                b = it * 2 + u
                dve.wait_ge(s_dn, spb * (b + 1))
                src = ps_out[u][:, :].rearrange("p (k b t) -> p b k t", k=KD, b=BLK)
                if is_shared:
                    a = acc[:, ds(b * BLK, BLK), :, :]
                    nc.vector.tensor_tensor(a, a, src, ALU.add).then_inc(s_y, 1)
                    return
                slot0 = (b - 2 * n_sh) * BLK
                wait(dve, s_add, slot0)
                ys = y.rearrange("p (b k t) -> p b k t", b=BLK, k=KD)
                w = wslot[:, ds(slot0, BLK)].unsqueeze(2).broadcast_to([P, BLK, TOK])
                for k in range(KD):
                    m = nc.vector.tensor_tensor(ys[:, :, k, :], src[:, :, k, :], w, ALU.mult)
                m.then_inc(s_y, 1)

            split_gu(0, 0)
            if layer == 2:
                nc.vector.tensor_copy(mem["bdn_b"], banks[6][:, 0:KD * NB].rearrange("p (k b) -> p b k", k=KD))\
                    .then_inc(s_bdn, 1)
                resplit_lo(nc.vector, mem, s_xhi, s_xlo, DVE_PIECES)
                dve.wait_ge(s_btab, 16)
            split_dn(0, 0)
            split_gu(0, 1)
            expert = [None]

            def body(it, last, prev_shared, now_shared):
                for s in range(spi):
                    t, p = it * spi + s, s % 2
                    if layer == 2 and s % spb == 0:
                        expert[0] = dve.value_load(eblk[0:1, ds(it * 2 + s // spb, 1)],
                                                   min_val=0, max_val=NE - 1)
                    dve.wait_ge(s_gel, t + 1)
                    dve.wait_ge(s_up, t + 1)
                    wait(dve, s_alo, t)
                    if layer == 1:
                        nc.vector.tensor_tensor(act1, ps_up[p][:, :], gel[:, p, :],
                                                ALU.mult).then_inc(s_act, 1)
                    else:
                        for c in range(2):
                            bias = btab[:, ds(expert[0] * 4 + NE * 4 + (s % spb) * 2 + c, 1)]
                            m = nc.vector.scalar_tensor_tensor(
                                act1[:, c * BT:(c + 1) * BT], ps_up[p][:, c * BT:(c + 1) * BT], bias,
                                gel[:, p, c * BT:(c + 1) * BT], ALU.add, ALU.mult)
                        m.then_inc(s_act, 1)
                    if not (last and s + 2 >= spi):
                        split_gu(it + (s + 2) // spi, (s + 2) % spi)
                    dve.wait_ge(s_ahi, t + 1)
                    nc.vector.tensor_tensor(ahl[:, p, 1, :], act1, ahl[:, p, 0, :].bitcast(F32),
                                            ALU.subtract).then_inc(s_alo, 1)
                    if not (last and s + 1 >= spi):
                        split_dn(it + (s + 1) // spi, (s + 1) % spi)
                    if s == spb:
                        output(it, 0, now_shared)
                    elif s == 0 and not (isinstance(it, int) and it == 0):
                        output(it - 1, 1, prev_shared)
                if last:
                    output(it, 1, now_shared)

            loop(dve, body)


def layer3(nc, sem, mem, banks, bias3, out_tok):
    xg, acc, gel, wbot, ysel, bias3_b = (mem[k] for k in ("xg", "acc", "gel", "wbot", "ysel", "bias3_b"))
    parts = mem["parts"][:, :].rearrange("p (j t) -> p j t", t=P)
    ps_b, ps_o = banks[0:4], banks[4:6]
    PB = CH // (SL * GB)
    NBK = KD * D // SL // PB
    HALF = GB // 2
    assert NBK == 16 and NG == 4

    s_xhi = sem("s_xhi_3")
    s_xlo = sem("s_xlo_3")
    s_b = sem("s_b")
    s_bhi = sem("s_bhi")
    s_blo = sem("s_blo")
    s_p = sem("s_p")
    s_bias3 = sem("s_bias3")
    s_o = sem("s_o")
    s_out = [sem(f"s_out_{u}") for u in range(2)]

    def group(eng, g, body):
        if g in (0, NG - 1):
            for r in range(2):
                body(g, r)
        else:
            with eng.Fori(0, 2) as r:
                body(g, r)

    def tokens(ap):
        return ap.rearrange("p k (b t) -> p k b t", b=BLK)

    with nc.Block() as block:
        @block.tensor
        def _(pe):
            mm = nc.tensor.matmul

            def build(g, m, e):
                n = g * NBK + m
                wait(pe, s_blo, n - 3)
                for j in range(PB):
                    for v in range(PARTS):
                        last = mm(ps_b[e][:, j * SL * GB:(j + 1) * SL * GB],
                                  parts[0:ROWS3, ds(m * PB + j, 1), :].rearrange("p a t -> p (a t)"),
                                  ysel[0:ROWS3, v, g, :, :].rearrange("p s b -> p (s b)"),
                                  start=v == 0, stop=v == PARTS - 1)
                last.then_inc(s_b, 1)

            for m in range(NBK):
                build(0, m, m % 4)

            def body(g, r):
                for q in range(4):
                    if g + 1 < NG:
                        for e in range(2):
                            build(g + 1, r * 8 + 2 * q + e, (2 * q + e) % 4)
                    pair, tile, u = 8 * g + 4 * r + q, 4 * g + 2 * r + q // 2, q // 2
                    if q == 0:
                        pe.wait_ge(s_blo, NBK * (g + 1))
                    if q % 2 == 0:
                        pe.wait_ge(s_xlo, tile + 1)
                    wait(pe, s_o, pair - 1)
                    for b in range(2):
                        at = ((q % 2) * 2 + b) * TOK
                        w = [wbot[:, g % 2, ds(r * HALF + 2 * q + b, 1), h, :].rearrange("p a o -> p (a o)")
                             for h in range(2)]
                        for k in range(KD):
                            m = split3(mm, ps_o[q % 2][0:TOK, b * D:(b + 1) * D],
                                       xg[:, u, k, at:at + TOK], xg[:, u, KD + k, at:at + TOK],
                                       w[0][:, k * D:(k + 1) * D], w[1][:, k * D:(k + 1) * D],
                                       start=k == 0, stop=k == KD - 1)
                    m.then_inc(s_p, 1)

            for g in range(NG):
                group(pe, g, body)

        def built(e):
            return ps_b[e][:, :].rearrange("p (o b) -> p b o", b=GB)

        def mixed(g, m, h):
            return wbot[:, g % 2, :, h, ds(m * PB * SL, PB * SL)]

        @block.scalar
        def _(se):
            def tile_hi(tile, u):
                wait(se, s_p, 2 * tile - 2)
                se.activation(tokens(xg[:, u, 0:KD, :]), acc[:, ds(tile * BLK, BLK), :, :]
                              .rearrange("p b k t -> p k b t"), ACT.Copy).then_inc(s_xhi, 1)

            def hi(g, m, e):
                se.wait_ge(s_b, g * NBK + m + 1)
                se.activation(mixed(g, m, 0), built(e), ACT.Copy).then_inc(s_bhi, 1)

            for m in range(NBK):
                hi(0, m, m % 4)
            tile_hi(0, 0)

            def body(g, r):
                for q in range(4):
                    if g + 1 < NG:
                        if q == 0:
                            wait(se, s_p, 8 * g)
                        for e in range(2):
                            hi(g + 1, r * 8 + 2 * q + e, (2 * q + e) % 4)
                    if q % 2 == 0 and not (g == NG - 1 and r == 1 and q == 2):
                        tile_hi(4 * g + 2 * r + q // 2 + 1, 1 - q // 2)

            for g in range(NG):
                group(se, g, body)

        @block.gpsimd
        def _(pool):
            def tile_lo(tile, u):
                pool.wait_ge(s_xhi, tile + 1)
                pool.tensor_tensor(tokens(xg[:, u, KD:, :]), acc[:, ds(tile * BLK, BLK), :, :]
                                   .rearrange("p b k t -> p k b t"),
                                   tokens(xg[:, u, 0:KD, :].bitcast(F32)), ALU.subtract).then_inc(s_xlo, 1)

            with pool.Fori(0, NB // BLK // 2) as i:
                for u in range(2):
                    tile_lo(2 * i + u, u)

        @block.vector
        def _(dve):
            def lo(g, m, e):
                dve.wait_ge(s_bhi, g * NBK + m + 1)
                nc.vector.tensor_tensor(mixed(g, m, 1), built(e), mixed(g, m, 0).bitcast(F32),
                                        ALU.subtract).then_inc(s_blo, 1)

            for m in range(NBK):
                lo(0, m, m % 4)
            dve.wait_ge(s_bias3, 16)

            def body(g, r):
                for q in range(4):
                    if g + 1 < NG:
                        for e in range(2):
                            lo(g + 1, r * 8 + 2 * q + e, (2 * q + e) % 4)
                    pair = 8 * g + 4 * r + q
                    dve.wait_ge(s_p, pair + 1)
                    wait(dve, s_out[q % 2], 16 * (4 * g + 2 * r + q // 2))
                    nc.vector.tensor_tensor(
                        gel[0:TOK, q % 2, :].rearrange("p (b o) -> p b o", b=2),
                        ps_o[q % 2][0:TOK, :].rearrange("p (b o) -> p b o", b=2),
                        bias3_b[0:TOK, :].unsqueeze(1).broadcast_to([TOK, 2, D]), ALU.add).then_inc(s_o, 1)

            for g in range(NG):
                group(dve, g, body)

        @block.sync
        def _(sp):
            sp.dma_start(bias3_b[:, :], bias3).then_inc(s_bias3, 16)
            with sp.Fori(0, NB // 4) as i:
                for u in range(2):
                    pair = 2 * i + u
                    sp.wait_ge(s_o, pair + 1)
                    sp.dma_start(out_tok[ds(pair * 2, 2), :, :].rearrange("b t o -> t b o"),
                                 gel[0:TOK, u, :].rearrange("p (b o) -> p b o", b=2)).then_inc(s_out[u], 16)
            for u in range(2):
                sp.wait_ge(s_out[u], 16 * (NB // 4))


def laid_out(i):
    def steps(first, second, down):
        n = down.shape[-2] // STEPH
        cols = [w.reshape(-1, KD, P, n, STEPH).transpose(0, 3, 2, 1, 4).reshape(-1, n, P, CH)
                for w in (first, second)]
        cols.append(down.reshape(-1, n, 2, P, D).transpose(0, 1, 3, 2, 4).reshape(-1, n, P, CH))
        return np.concatenate(cols, axis=3)

    def by_feature(a, chunks):
        return np.moveaxis(a.reshape(a.shape[:-1] + (chunks, P)), -1, 0).reshape(P, -1)

    w_base_t = i["L0_cond_W_base"].T.reshape(KD, P, D).transpose(1, 0, 2).reshape(P, CH)
    as_t = i["L0_cond_As"].reshape(P, KD, P).transpose(2, 1, 0).reshape(P, D)
    bs_t = i["L0_cond_Bs"].transpose(0, 2, 1).reshape(P, D)
    cond = i["cond_8"]

    def by_part(w, eye):
        w = w.reshape(-1, D // SL, SL, KD, P).transpose(2, 0, 3, 1, 4)
        w = np.broadcast_to(w, (PARTS, SL, NE) + w.shape[2:]).reshape(EYE, COL3)
        eye = eye.reshape(D // SL, SL, KD, P).transpose(1, 2, 0, 3).reshape(SL, COL3)
        return np.concatenate([w, eye])

    slices = np.concatenate([np.tile(np.repeat(np.arange(SL), NE), PARTS), np.arange(SL),
                             np.full(P - ROWS3, -1)])
    tr = lambda a: a.transpose(0, 2, 1)
    return {
        "x": i["x"].reshape(NB, TOK, KD, P).transpose(3, 0, 2, 1),
        "cond": cond,
        "w0": np.concatenate([w_base_t, as_t, bs_t], axis=1),
        "wexp": np.repeat(cond.T, R_LORA, axis=0),
        "yrep": np.concatenate([np.tile(cond.T, (PARTS * SL, 1)), np.ones((P - EYE, NB), cond.dtype)]),
        "delta": (slices[:, None] == np.arange(SL)).astype(np.float32),
        "w1": np.concatenate([
            steps(i["L1_cond_skill_gate"], i["L1_cond_skill_up"], i["L1_cond_skill_down"]),
            steps(i["L1_cond_shared_gate"], i["L1_cond_shared_up"], i["L1_cond_shared_down"])]),
        "w2": steps(tr(i["L2_cond_W_up"]), tr(i["L2_cond_W_gate"]), tr(i["L2_cond_W_down"])),
        "btab": np.concatenate([by_feature(i["L2_cond_b_up"], 4), by_feature(i["L2_cond_b_gate"], 4)], axis=1),
        "bias0": by_feature(i["L0_cond_b_base"], KD),
        "bdown2": i["L2_cond_b_down"],
        "weight3": by_part(i["L3_cond_weight"], np.eye(D, dtype=np.float32)),
        "mask3": by_part(i["L3_cond_mask"][None], np.ones((D, D), np.float32)),
        "bias3": np.broadcast_to(i["L3_cond_bias"], (P, D)),
    }


def kernel(**inputs):
    import concourse.bacc as bacc
    from concourse.bass_utils import run_bass_kernel_spmd

    nc = bacc.Bacc("TRN2", target_bir_lowering=False, num_devices=1)
    arrays, d = {}, {}
    for name, a in laid_out({k: np.asarray(v) for k, v in inputs.items()}).items():
        a = np.ascontiguousarray(a)
        arrays[f"in_{name}"] = a
        d[name] = nc.dram_tensor(f"in_{name}", a.shape, mybir.dt.from_np(a.dtype), kind="ExternalInput").ap()
    out = nc.dram_tensor("out_0", (NB, TOK, D), F32, kind="ExternalOutput").ap()
    d["out"] = out
    build(nc, d)
    r = run_bass_kernel_spmd(nc, [arrays], core_ids=[0])
    return r.results[0]["out_0"]
```

```python
from contextlib import ExitStack

import numpy as np

import concourse.bass as bass
from concourse import mybir

ALU = mybir.AluOpType
ACT = mybir.ActivationFunctionType
AX_X = mybir.AxisListType.X
F32 = mybir.dt.float32
F32R = mybir.dt.float32r
BF16 = mybir.dt.bfloat16
I32 = mybir.dt.int32
U32 = mybir.dt.uint32
ds = bass.ds

P = 128
NB, TOK, D = 64, 64, 256
NE = 8
KD = D // P
BLK = 4
BT = BLK * TOK
CH = 2 * BT
I1 = 1024
H2 = 512
STEPH = 256
WCOL = 3 * CH
RAWS = 4
N_SHARED = NB // BLK
N_TOP2 = (2 * NB + NE * (BLK - 1)) // BLK
N_TOP1 = (NB + NE * (BLK - 1)) // BLK
SLOTS1, SLOTS2 = N_TOP2 * BLK, N_TOP1 * BLK
assert N_SHARED % 2 == 0 and N_TOP2 % 2 == 0 and N_TOP1 % 2 == 0
assert I1 == 4 * STEPH and H2 == 2 * STEPH
assert RAWS == I1 // STEPH
R_LORA = 16
SCALING = 2.0
N_TILE0 = NB // BLK
NBIAS = NE * (2 * 4 + 2)
GB = 16
NG = NB // GB
SL = 4
ROWP = SL * NE
PASSES = ((0, 0, 0, 1), (None, 1, 2, None))
assert 4 * ROWP == P
BAND = P - SL
COL3 = KD * D // SL * P
STAGE = 512
QUARTERS = P // ROWP
N_STAGE = COL3 // QUARTERS // STAGE
PIECE_STEPS = 5
PIECE_DMAS = (P // ROWP) * QUARTERS


def wait(eng, sem, value):
    if not isinstance(value, int) or value > 0:
        eng.wait_ge(sem, value)


def rounds(eng, n, body):
    body(0, False)
    with eng.Fori(1, n - 1) as i:
        body(i, False)
    body(n - 1, True)


def build(nc, d):
    with ExitStack() as whole:
        def sem(name):
            return whole.enter_context(nc.semaphore(name))

        def into(stack):
            return lambda name, shape, dt=F32: stack.enter_context(nc.sbuf_tensor(name, shape, dt))

        sb = into(whole)
        mem = dict(
            acc=sb("acc", [P, NB, KD, TOK]),
            xg=sb("xg", [P, 2, 2 * KD, BT], F32R),
            gel=sb("gel", [P, 2, CH]),
            parts=sb("parts", [P, COL3], BF16),
            xhl=sb("xhl", [P, NB, 2 * KD, TOK], F32R),
            ysel=sb("ysel", [P, len(PASSES), NG, SL, GB], BF16),
            band=sb("band", [P, BAND + P + SL * GB], BF16),
        )
        banks = [whole.enter_context(nc.psum_tensor(f"bank{i}", [P, CH], F32)) for i in range(8)]
        s_raw = {layer: [sem(f"s_raw{r}_{layer}") for r in range(RAWS)] for layer in (1, 2)}

        ahead = {name: sem(f"s_{name}") for name in
                 ("whi", "wlo", "dhi", "dlo", "whi2", "wlo2", "dhi2", "dlo2", "b0", "b")}

        with ExitStack() as phase:
            sb = into(phase)
            stage = sb("stage", [P, 2, STAGE])
            mem.update(
                raw=sb("raw", [P, RAWS, WCOL]),
                whl=sb("whl", [P, 2, 2, WCOL], F32R),
                y=sb("y", [P, CH]),
                ahl=sb("ahl", [P, 2, 2, CH], F32R),
                stage=stage,
                zero=sb("zero", [P, 1]),
                piece=[sb("last", [P, STAGE], BF16)[:, :], stage[:, 1, STAGE // 2:].bitcast(BF16),
                       stage[:, 1, 0:STAGE // 2].bitcast(BF16)],
                btab=stage[:, 1, 0:NBIAS],
                xa=stage[:, 0, :],
                wslot1=sb("wslot1", [P, SLOTS1]),
                wslot2=sb("wslot2", [P, SLOTS2]),
                bslot1=sb("bslot1", [1, SLOTS1], I32),
                bslot2=sb("bslot2", [1, SLOTS2], I32),
                eblk1=sb("eblk1", [1, N_TOP2], I32),
                eblk2=sb("eblk2", [1, N_TOP1], I32),
            )
            layer0(nc, sem, mem, banks, d, s_raw, ahead)
            mlp(nc, sem, mem, banks, d, 1, s_raw, ahead)
            mlp(nc, sem, mem, banks, d, 2, s_raw, ahead)

        with ExitStack() as phase:
            sb = into(phase)
            mem.update(
                wodd=sb("wodd", [P, GB, 2, KD * D], F32R),
                bias3_b=sb("bias3_b", [P, D]),
            )
            layer3(nc, sem, mem, banks, ahead["b"], d["bias3"], d["out"])


def load_step(sp, mem, wts, s_raw, expert, q, slot):
    sp.dma_start(mem["raw"][:, slot, :], wts[ds(expert, 1), q].rearrange("e p w -> p (e w)"))\
        .then_inc(s_raw[slot], 16)


def layer0(nc, sem, mem, banks, d, s_raw, ahead):
    ahl, acc, xhl, whl, ysel = (mem[k] for k in ("ahl", "acc", "xhl", "whl", "ysel"))
    W_OFF, A_OFF, B_OFF = 0, CH, CH + D
    hs = [mem["y"][:, u * BT:(u + 1) * BT] for u in range(2)]
    hshl = [ahl[:, u, :, 0:BT] for u in range(2)]
    ps_h, ps_y, b7 = banks[0:2], banks[2:4], banks[7]
    w0 = mem["gel"][:, :, :].rearrange("p u w -> p (u w)")
    work = mem["raw"][:, 2:, :].rearrange("p s w -> p (s w)")
    at = [0]

    def rb(parts, *shape, dt=F32):
        n = int(np.prod(shape))
        view = work[0:parts, at[0]:at[0] + n]
        at[0] += n
        assert at[0] <= (RAWS - 2) * WCOL
        if dt is not F32:
            view = view.bitcast(dt)
        if len(shape) == 2:
            view = view.rearrange("p (a b) -> p a b", a=shape[0])
        if len(shape) == 3:
            view = view.rearrange("p (a b c) -> p a b c", a=shape[0], b=shape[1])
        return view

    cnd = rb(NB, NE)
    bias0 = rb(P, KD)
    wexp = rb(P, NB)
    top = rb(NB, 8)
    topi = rb(NB, 8, dt=U32)
    topf = rb(NB, 8)
    ntop = rb(NB, 1)
    ex = rb(NB, 8)
    prob = rb(NB, 12)
    hot = rb(NB, 3, NE)
    iota_e = rb(NB, NE)
    tri = rb(NB, NB)
    ones = rb(NB, P)
    iota_b = rb(NB, P)
    iota_s = rb(NB, SLOTS1)
    icnt = rb(P, 2, NE, dt=I32)
    run = rb(P, 3, 2, NE)
    first = rb(P, 2, NE)
    rank = rb(NB, 2, NE)
    pos = rb(NB, 2, NE)
    hpos = rb(NB, 3, NE)
    onehot = rb(NB, 2 * SLOTS1 + SLOTS2)
    wb = rb(NB, 2, P)
    iota4 = rb(1, N_TOP2)
    ended = rb(1, N_TOP2, NE)
    n_ended = rb(1, N_TOP2)
    yrep = rb(P, NB)
    ypart = rb(P, NB // 2).bitcast(BF16)
    band32 = rb(P, BAND + P + SL * GB)
    delta = rb(P, SL)

    s_const = sem("s_const")
    s_cond = sem("s_cond")
    s_small = sem("s_small")
    s_w0 = [sem(f"s_w0_{b}") for b in range(2)]
    s_route = sem("s_route")
    s_table = sem("s_table")
    s_exp = sem("s_exp")
    s_sel = sem("s_sel")
    s_w0hi = sem("s_w0hi")
    s_w0lo = sem("s_w0lo")
    s_x = sem("s_x")
    s_x0hi = sem("s_x0hi")
    s_x0lo = sem("s_x0lo")
    s_h = sem("s_h")
    s_hs = sem("s_hs")
    s_hshi = sem("s_hshi")
    s_hslo = sem("s_hslo")
    s_y = sem("s_y")
    s_x1 = sem("s_x1")
    s_x1hi = sem("s_x1hi")
    s_x1lo = sem("s_x1lo")
    s_ysel = sem("s_ysel")
    mark = {}

    with nc.Block() as block:
        @block.sync
        def _(sp):
            sp.dma_start(cnd, d["cond"]).then_inc(s_cond, 16)
            sp.dma_start(w0[:, CH:], d["w0"][:, CH:]).then_inc(s_w0[1], 16)
            def load_x(i):
                wait(sp, s_x, 16 * i)
                sp.dma_start(acc[:, ds(2 * BLK * i, 2 * BLK), :, :].rearrange("p b k t -> p (b k t)"),
                             d["x"][:, ds(2 * BLK * i, 2 * BLK), :, :].rearrange("p b k t -> p (b k t)"))\
                    .then_inc(s_x, 16)

            load_x(0)
            sp.dma_start(w0[:, :CH], d["w0"][:, :CH]).then_inc(s_w0[0], 16)
            small = ((bias0, d["bias0"]), (wexp, d["wexp"]), 
                     (yrep, d["yrep"]), (delta, d["delta"]), (band32, d["band"]))
            for dst, src in small:
                sp.dma_start(dst, src).then_inc(s_small, 16)
            mark["small"] = 16 * len(small)
            with sp.Fori(1, N_TILE0 // 2) as i:
                load_x(i)

            for r in range(2):
                load_step(sp, mem, d["w1"], s_raw[1], NE, r, r)
            sp.wait_ge(s_x1, N_TILE0)
            sp.wait_ge(s_route, N_ROUTE)
            sp.wait_ge(s_ysel, N_YSEL)
            for r in range(2, RAWS):
                load_step(sp, mem, d["w1"], s_raw[1], NE, r, r)

        @block.gpsimd
        def _(pool):
            pool.memset(tri, 0.0).then_inc(s_const, 1)
            pool.memset(ones, 1.0).then_inc(s_const, 1)
            pool.memset(mem["zero"][:, :], 0.0)
            for dst, pattern, channel in ((iota_e, [[1, NE]], 0), (iota_b, [[0, P]], 1),
                                          (iota_s, [[1, SLOTS1]], 0), (iota4, [[BLK, N_TOP2]], 0)):
                pool.iota(dst, pattern, base=0, channel_multiplier=channel,
                          allow_small_or_imprecise_dtypes=True).then_inc(s_const, 1)
            pool.wait_ge(s_const, 6)
            pool.affine_select(out=tri, in_=tri, compare_op=ALU.is_ge, fill=1.0,
                               base=0, pattern=[[-1, NB]], channel_multiplier=1).then_inc(s_const, 1)

            steps = [0]

            def step(ins):
                steps[0] += 1
                ins.then_inc(s_table, 1)
                pool.wait_ge(s_table, steps[0])

            pool.wait_ge(s_route, ROUTED)
            for shift, a, b in ((1, 0, 1), (2, 1, 2), (4, 2, 1)):
                step(pool.tensor_copy(run[:, b, :, 0:shift], run[:, a, :, 0:shift]))
                step(pool.tensor_tensor(run[:, b, :, shift:], run[:, a, :, shift:],
                                        run[:, a, :, :NE - shift], ALU.add))
            end = run[:, 1]
            step(pool.tensor_tensor(first, end, run[:, 0], ALU.subtract))
            step(pool.tensor_tensor(pos, rank, first[:NB], ALU.add))
            for k in range(2):
                step(pool.tensor_tensor(hpos[:, k, :], hot[:, k, :], pos[:, 0, :], ALU.mult))
            step(pool.tensor_tensor(hpos[:, 2, :], hot[:, 0, :], pos[:, 1, :], ALU.mult))
            for n in (4, 2, 1):
                step(pool.tensor_tensor(hpos[:, :, 0:n], hpos[:, :, 0:n], hpos[:, :, n:2 * n], ALU.add))
            assert steps[0] == N_TABLE

            steps[0] = 0

            def ystep(ins):
                steps[0] += 1
                ins.then_inc(s_ysel, 1)
                pool.wait_ge(s_ysel, steps[0])

            pool.wait_ge(s_small, mark["small"])
            ystep(pool.memset(ysel[:, :, :, :, :], 0.0))
            ystep(pool.tensor_copy(mem["band"][:, :], band32))
            for part, v, first_row, last_row in ((0, 0, 0, 3), (1, 0, 3, 4), (1, 1, 0, 2), (2, 1, 2, 3)):
                if (part, v) in ((1, 0), (2, 1)):
                    ystep(pool.tensor_copy(ypart, yrep))
                    ystep(pool.tensor_tensor(yrep, yrep, ypart, ALU.subtract))
                rows = slice(first_row * ROWP, last_row * ROWP)
                n = rows.stop - rows.start
                for s in range(SL):
                    ystep(pool.tensor_tensor(
                        ysel[rows, v, :, s, :], yrep[rows].rearrange("p (g b) -> p g b", g=NG),
                        delta[rows, s:s + 1].unsqueeze(2).broadcast_to([n, NG, GB]), ALU.mult))
            ystep(pool.memset(ysel[0:ROWP, 1, :, :, :], 0.0))

            def split_out(t):
                pool.wait_ge(s_x1hi, t + 1)
                pool.tensor_tensor(xhl[:, ds(t * BLK, BLK), KD:, :], acc[:, ds(t * BLK, BLK), :, :],
                                   xhl[:, ds(t * BLK, BLK), 0:KD, :].bitcast(F32),
                                   ALU.subtract).then_inc(s_x1lo, 1)

            with pool.Fori(0, N_TILE0 - 1) as t:
                split_out(t)

        @block.vector
        def _(dve):
            steps = [0]

            def step(ins):
                steps[0] += 1
                ins.then_inc(s_route, 1)
                dve.wait_ge(s_route, steps[0])

            dve.wait_ge(s_cond, 16)
            step(nc.vector.max(top, cnd))
            step(nc.vector.tensor_scalar(ntop, top[:, 0:1], -1.0, None, ALU.mult))
            step(nc.vector.max_index(topi, top, cnd))
            step(nc.vector.tensor_copy(topf, topi))
            dve.wait_ge(s_const, 7)
            for k in range(2):
                step(nc.vector.tensor_scalar(hot[:, k, :], iota_e, topf[:, k:k + 1], None, ALU.is_equal))
            step(nc.vector.tensor_tensor(hot[:, 2, :], hot[:, 0, :], hot[:, 1, :], ALU.add))
            mark["hot"] = steps[0]

            def tile_in(t):
                dve.wait_ge(s_x0hi, t + 1)
                nc.vector.tensor_tensor(xhl[:, ds(t * BLK, BLK), KD:, :], acc[:, ds(t * BLK, BLK), :, :],
                                        xhl[:, ds(t * BLK, BLK), 0:KD, :].bitcast(F32),
                                        ALU.subtract).then_inc(s_x0lo, 1)

            for b in (1, 0):
                dve.wait_ge(s_w0hi, 2 - b)
                nc.vector.tensor_tensor(whl[:, 1, 1, b * CH:(b + 1) * CH], w0[:, b * CH:(b + 1) * CH],
                                        whl[:, 1, 0, b * CH:(b + 1) * CH].bitcast(F32),
                                        ALU.subtract).then_inc(s_w0lo, 1)
                tile_in(1 - b)
            dve.wait_ge(s_exp, 1)
            step(nc.vector.reduce_sum(prob[:, 0:1], ex, AX_X))
            step(nc.vector.reciprocal(prob[:, 1:2], prob[:, 0:1]))
            step(nc.vector.tensor_scalar(prob[:, 2:4], ex[:, 0:2], prob[:, 1:2], None, ALU.mult))
            step(nc.vector.tensor_tensor(prob[:, 4:5], prob[:, 2:3], prob[:, 3:4], ALU.add))
            step(nc.vector.reciprocal(prob[:, 5:6], prob[:, 4:5]))
            step(nc.vector.tensor_scalar(prob[:, 6:8], prob[:, 2:4], prob[:, 5:6], None, ALU.mult))
            step(nc.vector.tensor_scalar(prob[:, 8:10], prob[:, 6:8], 1.0 - 1.0 / 12, None, ALU.mult))
            step(nc.vector.scalar_tensor_tensor(prob[:, 10:12], prob[:, 6:8], 1.0 / 12, prob[:, 8:10],
                                                ALU.mult, ALU.add))
            dve.wait_ge(s_small, mark["small"])
            step(nc.vector.tensor_scalar(wexp, wexp, SCALING, None, ALU.mult))
            for k in range(2):
                step(nc.vector.tensor_scalar(wb[:, k, :], ones, prob[:, 10 + k:11 + k], None, ALU.mult))
            dve.wait_ge(s_sel, 1)
            step(nc.vector.tensor_scalar(icnt, b7[:, 16:32].rearrange("p (a e) -> p a e", a=2),
                                         float(BLK - 1), None, ALU.add))
            step(nc.vector.tensor_scalar(icnt, icnt, BLK.bit_length() - 1, BLK.bit_length() - 1,
                                         ALU.logical_shift_right, ALU.logical_shift_left))
            step(nc.vector.tensor_copy(run[:, 0], icnt))
            step(nc.vector.tensor_copy(rank, b7[:NB, 0:16].rearrange("p (a e) -> p a e", a=2)))
            assert steps[0] == ROUTED

            def sum_out(t, u):
                dve.wait_ge(s_y, t + 1)
                for c in range(KD):
                    a = acc[:, ds(t * BLK, BLK), c, :]
                    m = nc.vector.scalar_tensor_tensor(
                        a, ps_y[u][:, c * BT:(c + 1) * BT].rearrange("p (b t) -> p b t", b=BLK),
                        bias0[:, c:c + 1], a, ALU.add, ALU.add)
                m.then_inc(s_x1, 1)

            def pair(i, last):
                for u in range(2):
                    t = 2 * i + u
                    inner = not (isinstance(t, int) and t == 0)
                    dve.wait_ge(s_h, t + 1)
                    w = wexp[:, ds(t * BLK, BLK)].unsqueeze(2).broadcast_to([P, BLK, TOK])
                    nc.vector.tensor_tensor(hs[u].rearrange("p (b t) -> p b t", b=BLK),
                                            ps_h[u][:, 0:BT].rearrange("p (b t) -> p b t", b=BLK), w,
                                            ALU.mult).then_inc(s_hs, 1)
                    if inner:
                        sum_out(t - 1, 1 - u)
                    dve.wait_ge(s_hshi, t + 1)
                    nc.vector.tensor_tensor(hshl[u][:, 1, :], hs[u], hshl[u][:, 0, :].bitcast(F32),
                                            ALU.subtract).then_inc(s_hslo, 1)
                    if not last:
                        tile_in(t + 2)
                if last:
                    sum_out(t, 1)

            pair(0, False)
            dve.wait_ge(s_table, N_TABLE)
            for k in range(3):
                width = SLOTS1 if k < 2 else SLOTS2
                step(nc.vector.tensor_scalar(onehot[:, k * SLOTS1:k * SLOTS1 + width], iota_s[:, :width],
                                             hpos[:, k, 0:1], None, ALU.is_equal))
            mark["onehot"] = steps[0]
            for a, n, tab in ((0, N_TOP2, "eblk1"), (1, N_TOP1, "eblk2")):
                step(nc.vector.tensor_tensor(ended[:, :n, :], iota4[:, :n].unsqueeze(2).broadcast_to([1, n, NE]),
                                             run[0:1, 1, a, :].unsqueeze(1).broadcast_to([1, n, NE]),
                                             ALU.is_ge))
                step(nc.vector.reduce_sum(n_ended[:, :n], ended[:, :n, :], AX_X))
                step(nc.vector.tensor_scalar(mem[tab][:, :], n_ended[:, :n], float(NE - 1), None, ALU.min))
            pair(1, False)
            dve.wait_ge(s_sel, 2)
            step(nc.vector.tensor_copy(mem["wslot1"][:, :], b7[:, 0:SLOTS1]))
            step(nc.vector.tensor_copy(mem["bslot1"][:, :], b7[0:1, 160:160 + SLOTS1]))
            step(nc.vector.tensor_copy(mem["wslot2"][:, :], b7[:, 320:320 + SLOTS2]))
            step(nc.vector.tensor_copy(mem["bslot2"][:, :], b7[0:1, 416:416 + SLOTS2]))
            assert steps[0] == N_ROUTE
            with dve.Fori(2, N_TILE0 // 2 - 1) as i:
                pair(i, False)

            def first_lo(o, hi, lo):
                dve.wait_ge(ahead[hi], 1)
                nc.vector.tensor_tensor(whl[:, 0, 1, o], mem["raw"][:, 0, o], whl[:, 0, 0, o].bitcast(F32),
                                        ALU.subtract).then_inc(ahead[lo], 1)

            first_lo(slice(0, 2 * CH), "whi", "wlo")
            pair(N_TILE0 // 2 - 1, True)
            first_lo(slice(2 * CH, WCOL), "dhi", "dlo")
            dve.wait_ge(s_x1hi, N_TILE0)
            t = slice((N_TILE0 - 1) * BLK, NB)
            nc.vector.tensor_tensor(xhl[:, t, KD:, :], acc[:, t, :, :], xhl[:, t, 0:KD, :].bitcast(F32),
                                    ALU.subtract).then_inc(s_x1lo, 1)

        @block.scalar
        def _(se):
            se.wait_ge(s_route, 2)
            se.activation(ex, top, ACT.Exp, bias=ntop[:, 0:1]).then_inc(s_exp, 1)
            def tile_in(t, n):
                se.wait_ge(s_x, 16 * n)
                se.activation(xhl[:, ds(t * BLK, BLK), 0:KD, :], acc[:, ds(t * BLK, BLK), :, :],
                              ACT.Copy).then_inc(s_x0hi, 1)

            for b in (1, 0):
                if b == 0:
                    tile_in(0, 1)
                se.wait_ge(s_w0[b], 16)
                se.activation(whl[:, 1, 0, b * CH:(b + 1) * CH], w0[:, b * CH:(b + 1) * CH],
                              ACT.Copy).then_inc(s_w0hi, 1)

            tile_in(1, 1)

            def tile_out(t, u):
                se.wait_ge(s_x1, t + 1)
                se.activation(xhl[:, ds(t * BLK, BLK), 0:KD, :], acc[:, ds(t * BLK, BLK), :, :],
                              ACT.Copy).then_inc(s_x1hi, 1)

            def pair(i, last):
                for u in range(2):
                    t = 2 * i + u
                    se.wait_ge(s_hs, t + 1)
                    wait(se, s_y, t - 1)
                    se.activation(hshl[u][:, 0, :], hs[u], ACT.Copy).then_inc(s_hshi, 1)
                    if not last:
                        tile_in(t + 2, i + 2)
                    if not (isinstance(t, int) and t == 0):
                        tile_out(t - 1, 1 - u)

            pair(0, False)
            with se.Fori(1, N_TILE0 // 2 - 1) as i:
                pair(i, False)

            def first_hi(o, hi):
                se.activation(whl[:, 0, 0, o], mem["raw"][:, 0, o], ACT.Copy).then_inc(ahead[hi], 1)

            se.wait_ge(s_raw[1][0], 16)
            first_hi(slice(0, 2 * CH), "whi")
            pair(N_TILE0 // 2 - 1, True)
            first_hi(slice(2 * CH, WCOL), "dhi")
            tile_out(N_TILE0 - 1, 1)

        @block.tensor
        def _(pe):
            mm = nc.tensor.matmul
            pe.wait_ge(s_const, 7)
            pe.wait_ge(s_route, mark["hot"])
            mm(b7[:NB, 0:8], tri, hot[:, 2, :], start=True, stop=True)
            mm(b7[:NB, 8:16], tri, hot[:, 0, :], start=True, stop=True)
            mm(b7[:, 16:24], ones, hot[:, 2, :], start=True, stop=True)
            mm(b7[:, 24:32], ones, hot[:, 0, :], start=True, stop=True).then_inc(s_sel, 1)

            def w(hl, o):
                return whl[:, 1, hl, o:o + P]

            def by_batch(ap):
                return ap.rearrange("p (b t) -> p b t", b=BLK)

            def tokens(t, k):
                return [xhl[:, ds(t * BLK, BLK), h * KD + k, :] for h in range(2)]

            def inner(t, u):
                pe.wait_ge(s_x0lo, t + 1)
                wait(pe, s_hs, t - 1)
                for k in range(KD):
                    o = A_OFF + k * P
                    m = split3(mm, by_batch(ps_h[u][:, 0:BT]), w(0, o), w(1, o), *tokens(t, k),
                               start=k == 0, stop=k == KD - 1)
                m.then_inc(s_h, 1)

            pe.wait_ge(s_w0lo, 1)
            inner(0, 0)
            pe.wait_ge(s_w0lo, 2)

            def pair(i, last):
                for u in range(2):
                    t = 2 * i + u
                    if not (last and u == 1):
                        inner(t + 1, 1 - u)
                    wait(pe, s_x1, t - 1)
                    for c in range(KD):
                        for k in range(KD):
                            o = W_OFF + k * D + c * P
                            split3(mm, by_batch(ps_y[u][:, c * BT:(c + 1) * BT]), w(0, o), w(1, o),
                                   *tokens(t, k), start=c == 0 and k == 0, stop=False,
                                   skip_group_check=True)
                    pe.wait_ge(s_hslo, t + 1)
                    for c in range(KD):
                        o = B_OFF + c * P
                        m = split3(mm, ps_y[u][:, c * BT:(c + 1) * BT], w(0, o), w(1, o), hshl[u][:, 0, :],
                                   hshl[u][:, 1, :], start=False, stop=True, skip_group_check=True)
                    m.then_inc(s_y, 1)

            pair(0, False)
            pe.wait_ge(s_route, mark["onehot"])
            for lhs, o in (((wb[:, 0, :], wb[:, 1, :]), 0), ((iota_b, iota_b), 160)):
                for k in range(2):
                    mm(b7[:, o:o + SLOTS1], lhs[k], onehot[:, k * SLOTS1:(k + 1) * SLOTS1],
                       start=k == 0, stop=k == 1)
            for lhs, o in ((ones, 320), (iota_b, 416)):
                last = mm(b7[:, o:o + SLOTS2], lhs, onehot[:, 2 * SLOTS1:], start=True, stop=True)
            last.then_inc(s_sel, 1)
            with pe.Fori(1, N_TILE0 // 2 - 1) as i:
                pair(i, False)
            pair(N_TILE0 // 2 - 1, True)


ROUTED = 22
N_ROUTE = ROUTED + 13
N_TABLE = 14
N_YSEL = 3 + 4 * SL + 4


def split3(mm, out, w_hi, w_lo, x_hi, x_lo, start, stop, **kw):
    mm(out, w_lo, x_hi, start=start, stop=False, **kw)
    mm(out, w_hi, x_lo, start=False, stop=False, **kw)
    return mm(out, w_hi, x_hi, start=False, stop=stop, **kw)


PB = CH // (SL * GB)
NBK = KD * D // SL // PB
assert NBK == 16 and NG == 4


def build_columns(mm, mem, g, m, bank, js):
    cols = mem["parts"][:, ds(m * PB * P, PB * P)]
    band = mem["band"]
    for j in js:
        k, o = (m * PB + j) * SL // D, (m * PB + j) * SL % D
        out = bank[:, j * SL * GB:(j + 1) * SL * GB]
        diagonal = o // P == k
        for v in range(len(PASSES)):
            last = mm(out, cols[:, j * P:(j + 1) * P], mem["ysel"][:, v, g, :, :].rearrange("p s b -> p (s b)"),
                      start=v == 0, stop=v == len(PASSES) - 1 and not diagonal)
        if diagonal:
            at = BAND - o % P
            last = mm(out, band[:, at:at + P], band[:, BAND + P:], start=False, stop=True)
    return last


def wbot(mem, g):
    if g % 2:
        return mem["wodd"][:, :, :, :]
    return mem["xhl"][:, :, :, :].rearrange("p b k t -> p (b k t)").rearrange(
        "p (b h o) -> p b h o", b=GB, h=2)


def built(bank):
    return bank[:, :].rearrange("p (o b) -> p b o", b=GB)


def mixed(mem, g, m, h):
    return wbot(mem, g)[:, :, h, ds(m * PB * SL, PB * SL)]


def mlp(nc, sem, mem, banks, d, layer, s_raws, ahead):
    raw, whl, xg, gel, y, ahl = (mem[k] for k in ("raw", "whl", "xg", "gel", "y", "ahl"))
    acc, xhl, btab = mem["acc"], mem["xhl"], mem["btab"]
    wslot, bslot, eblk = mem[f"wslot{layer}"], mem[f"bslot{layer}"], mem[f"eblk{layer}"]
    spb = 4 if layer == 1 else 2
    spi = 2 * spb
    n_sh = N_SHARED // 2 if layer == 1 else 0
    wts, s_raw = d[f"w{layer}"], s_raws[layer]
    n_it = n_sh + (N_TOP2 if layer == 1 else N_TOP1) // 2
    ps_gate, ps_up, ps_out = banks[0:2], banks[2:4], banks[4:6]
    act1 = banks[6]
    GU = 2 * CH

    L = f"_{layer}"
    s_whi, s_wlo, s_dhi, s_dlo = (ahead[name if layer == 1 else name + "2"]
                                  for name in ("whi", "wlo", "dhi", "dlo"))
    next_split = ((0, slice(0, 2 * CH), "whi2", "wlo2"), (0, slice(2 * CH, WCOL), "dhi2", "dlo2"),
                  (1, slice(0, 2 * CH), "whi2", "wlo2"))
    s_xg = sem("s_xg" + L)
    s_gate = sem("s_gate" + L)
    s_up = sem("s_up" + L)
    s_gel = sem("s_gel" + L)
    s_act = sem("s_act" + L)
    s_ahi = sem("s_ahi" + L)
    s_alo = sem("s_alo" + L)
    s_dn = sem("s_dn" + L)
    s_y = sem("s_y" + L)
    s_add = sem("s_add" + L)
    s_btab = sem("s_btab" + L)
    s_stage = sem("s_stage" + L)
    s_part = sem("s_part" + L)
    s_placed = sem("s_placed" + L)
    s_xa = sem("s_xa" + L)
    s_xahi = sem("s_xahi" + L)
    s_b0 = ahead["b0"]
    s_b0hi = sem("s_b0hi" + L)
    s_b0lo = sem("s_b0lo" + L)

    def loop(eng, body):
        body(0, False, bool(n_sh), bool(n_sh))
        if n_sh:
            with eng.Fori(1, n_sh) as i:
                body(i, False, True, True)
            body(n_sh, False, True, False)
        with eng.Fori(n_sh + 1, n_it - 1) as i:
            body(i, False, False, False)
        body(n_it - 1, True, False, False)

    def turns(it, s):
        return (it - n_sh) * (spi // RAWS) + s // RAWS + 1 + (1 if n_sh else 0)

    xa = mem["xa"].rearrange("p (b k t) -> p b k t", b=BLK, k=KD)
    per_xg = BLK if layer == 1 else 1

    def by_batch(ap):
        return ap.rearrange("p k (b t) -> p b k t", b=BLK)

    with nc.Block() as block:
        @block.sync
        def _(sp):
            def stage_piece(c):
                if not (isinstance(c, int) and c == 0):
                    sp.wait_ge(s_placed, 16 * PIECE_DMAS * c)
                for a, name in enumerate(("weight3", "mask3")):
                    sp.dma_start(mem["stage"][:, a, :], d[name][:, ds(c * STAGE, STAGE)])\
                        .then_inc(s_stage, 16)
                sp.wait_ge(s_part, PIECE_STEPS * (c + 1))
                for kind, part in enumerate((0, 1, 2, 2)):
                    for q in range(QUARTERS):
                        dst = mem["parts"][kind * ROWP:(kind + 1) * ROWP,
                                           q * (COL3 // QUARTERS):(q + 1) * (COL3 // QUARTERS)]
                        sp.dma_start(dst[:, ds(c * STAGE, STAGE)],
                                     mem["piece"][part][q * ROWP:(q + 1) * ROWP]).then_inc(s_placed, 16)

            def load(it, first=0):
                for s in range(first, spi):
                    t = it * spi + s
                    if s % spb == 0:
                        e = sp.value_load(eblk[0:1, ds((it - n_sh) * 2 + s // spb, 1)],
                                          min_val=0, max_val=NE - 1)
                    wait(sp, s_wlo, t - RAWS + 1)
                    wait(sp, s_dlo, t - RAWS + 1)
                    load_step(sp, mem, wts, s_raw, e, s % spb, s % RAWS)

            if layer == 1:
                stage_piece(0)
                with sp.Fori(1, N_STAGE) as c:
                    stage_piece(c)
                load(n_sh)
                with sp.Fori(n_sh + 1, n_it) as i:
                    load(i)
            else:
                sp.dma_start(btab, d["btab"]).then_inc(s_btab, 16)
                with sp.Fori(1, n_it) as i:
                    load(i)
            if layer == 1:
                for r in range(RAWS):
                    t = n_it * spi + r
                    if r % 2 == 0:
                        e = sp.value_load(mem["eblk2"][0:1, r // 2:r // 2 + 1], min_val=0, max_val=NE - 1)
                    sp.wait_ge(s_wlo, t - RAWS + 1)
                    sp.wait_ge(s_dlo, t - RAWS + 1)
                    load_step(sp, mem, d["w2"], s_raws[2], e, r % 2, r)

        @block.gpsimd
        def _(pool):
            def fetch(b, added):
                wait(pool, s_xg, b)
                wait(pool, s_add, BLK * added)
                for j in range(BLK):
                    batch = pool.value_load(bslot[0:1, ds(b * BLK + j, 1)], min_val=0, max_val=NB - 1)
                    pool.tensor_copy(mem["xa"][:, j * KD * TOK:(j + 1) * KD * TOK],
                                     acc[:, ds(batch, 1), :, :].rearrange("p b k t -> p (b k t)"))\
                        .then_inc(s_xa, 1)

            def x_lo(b, u):
                pool.wait_ge(s_xahi, b + 1)
                pool.wait_ge(s_xa, BLK * (b + 1))
                pool.tensor_tensor(by_batch(xg[:, u, KD:, :]), xa, by_batch(xg[:, u, 0:KD, :].bitcast(F32)),
                                   ALU.subtract).then_inc(s_xg, 1)

            def gather(it, u):
                b = it * 2 + u
                if not (isinstance(it, int) and it == n_sh):
                    wait(pool, s_up, spb * (b - 1))
                for j in range(BLK):
                    batch = pool.value_load(bslot[0:1, ds((b - 2 * n_sh) * BLK + j, 1)],
                                            min_val=0, max_val=NB - 1)
                    pool.tensor_copy(xg[:, u, :, j * TOK:(j + 1) * TOK],
                                     xhl[:, ds(batch, 1), :, :].rearrange("p b k t -> p (b k) t"))\
                        .then_inc(s_xg, 1)

            def add(it, u):
                b = it * 2 + u
                slot0 = (b - 2 * n_sh) * BLK
                pool.wait_ge(s_y, b + 1)
                for j in range(BLK):
                    batch = pool.value_load(bslot[0:1, ds(slot0 + j, 1)], min_val=0, max_val=NB - 1)
                    a = acc[:, ds(batch, 1), :, :].rearrange("p b k t -> p (b k t)")
                    wait(pool, s_add, slot0 + j)
                    pool.tensor_tensor(a, a, y[:, j * KD * TOK:(j + 1) * KD * TOK], ALU.add).then_inc(s_add, 1)

            def mask_and_split(c):
                w, mask = mem["stage"][:, 0, :], mem["stage"][:, 1, :]
                last, middle, leading = mem["piece"]
                zero = mem["zero"][:, :].broadcast_to([P, STAGE])
                pool.wait_ge(s_stage, 32 * (c + 1))
                for k, (out, in0, in1, op) in enumerate((
                        (w, w, mask, ALU.mult), (leading, w, zero, ALU.add),
                        (w, w, leading, ALU.subtract), (middle, w, zero, ALU.add),
                        (last, w, middle, ALU.subtract))):
                    wait(pool, s_part, PIECE_STEPS * c + k)
                    pool.tensor_tensor(out, in0, in1, op).then_inc(s_part, 1)

            def routed(i):
                for u in range(2):
                    gather(i, u)
                    add(i - 1, u)

            def routed2(i, last):
                for u in range(2):
                    b = 2 * i + u
                    x_lo(b, u)
                    if not (last and u == 1):
                        fetch(b + 1, b - 2)
                    add(i - 1, u)

            if layer == 1:
                for u in range(2):
                    gather(n_sh, u)
                mask_and_split(0)
                with pool.Fori(1, N_STAGE) as c:
                    mask_and_split(c)
                routed(n_sh + 1)
                with pool.Fori(n_sh + 2, n_it) as i:
                    routed(i)
            else:
                fetch(0, 0)
                x_lo(0, 0)
                fetch(1, 0)
                x_lo(1, 1)
                fetch(2, 0)
                routed2(1, False)
                with pool.Fori(2, n_it - 1) as i:
                    routed2(i, False)
                routed2(n_it - 1, True)
            for u in range(2):
                add(n_it - 1, u)

        @block.tensor
        def _(pe):
            mm = nc.tensor.matmul

            if layer == 2:
                for m in range(4, NBK):
                    pe.wait_ge(s_b0lo, m - 3)
                    build_columns(mm, mem, 0, m, banks[m % 4], range(PB)).then_inc(s_b0, 1)

            def project(it, s, is_shared):
                t, p, u = it * spi + s, s % 2, s // spb
                if s % spb == 0 and not is_shared:
                    pe.wait_ge(s_xg, per_xg * ((it - n_sh) * 2 + u + 1))
                pe.wait_ge(s_wlo, t + 1)
                for o, n, freed, done in ((0, p, s_gel, s_gate), (CH, 2 + p, s_act, s_up)):
                    bank = banks[n]
                    if layer == 2 and isinstance(t, int) and t < 2:
                        pe.wait_ge(s_b0lo, NBK - 4 + n + 1)
                    wait(pe, freed, t - 1)
                    for c in range(2):
                        for k in range(KD):
                            q = o + k * STEPH + c * P
                            out = bank[:, c * BT:(c + 1) * BT]
                            if is_shared:
                                out = out.rearrange("p (b t) -> p b t", b=BLK)
                                x = [xhl[:, ds((2 * it + u) * BLK, BLK), h * KD + k, :] for h in range(2)]
                            else:
                                x = [xg[:, u, h * KD + k, :] for h in range(2)]
                            m = split3(mm, out, whl[:, p, 0, q:q + P], whl[:, p, 1, q:q + P], *x,
                                       start=k == 0, stop=k == KD - 1)
                    m.then_inc(done, 1)

            def down(it, s):
                t, p, u = it * spi + s, s % 2, s // spb
                pe.wait_ge(s_alo, t + 1)
                pe.wait_ge(s_dlo, t + 1)
                first, last = s % spb == 0, s % spb == spb - 1
                if first:
                    wait(pe, s_y, it * 2 + u - 1)
                for c in range(2):
                    for k in range(KD):
                        q = GU + c * D + k * P
                        m = split3(mm, ps_out[u][:, k * BT:(k + 1) * BT], whl[:, p, 0, q:q + P],
                                   whl[:, p, 1, q:q + P], ahl[:, p, 0, c * BT:(c + 1) * BT],
                                   ahl[:, p, 1, c * BT:(c + 1) * BT], start=first and c == 0 and k == 0,
                                   stop=last and c == 1, skip_group_check=True)
                m.then_inc(s_dn, 1)

            def body(it, last, is_shared):
                for s in range(spi):
                    project(it, s, is_shared)
                    if s > 0:
                        down(it, s - 1)
                    elif not (isinstance(it, int) and it == 0):
                        down(it - 1, spi - 1)
                if last:
                    down(it, spi - 1)

            body(0, False, bool(n_sh))
            if n_sh:
                with pe.Fori(1, n_sh) as i:
                    body(i, False, True)
            with pe.Fori(max(n_sh, 1), n_it - 1) as i:
                body(i, False, False)
            body(n_it - 1, True, False)
            pe.wait_ge(s_gel, n_it * spi)
            pe.wait_ge(s_act, n_it * spi)
            if layer == 1:
                pe.wait_ge(s_placed, 16 * PIECE_DMAS * N_STAGE)
            for m in range(4):
                build_columns(mm, mem, layer - 1, m, banks[m], range(PB))\
                    .then_inc(ahead["b0" if layer == 1 else "b"], 1)

        @block.scalar
        def _(se):
            def split_gu(it, s, is_shared):
                t, p = it * spi + s, s % 2
                wait(se, s_up, t - 1)
                se.wait_ge(s_raw[s % RAWS], 16 if is_shared else 16 * turns(it, s))
                se.activation(whl[:, p, 0, 0:GU], raw[:, s % RAWS, 0:GU], ACT.Copy).then_inc(s_whi, 1)

            def split_dn(it, s):
                t, p = it * spi + s, s % 2
                wait(se, s_dn, t - 1)
                se.activation(whl[:, p, 0, GU:], raw[:, s % RAWS, GU:], ACT.Copy).then_inc(s_dhi, 1)

            def x_hi(b, u):
                wait(se, s_up, spb * (b - 1))
                se.wait_ge(s_xa, BLK * (b + 1))
                se.activation(by_batch(xg[:, u, 0:KD, :]), xa, ACT.Copy).then_inc(s_xahi, 1)

            def b0_hi(banks_m):
                for m in banks_m:
                    se.wait_ge(s_b0, m + 1)
                    se.activation(mixed(mem, 0, m, 0), built(banks[m % 4]), ACT.Copy).then_inc(s_b0hi, 1)

            if layer == 2:
                b0_hi(range(8))
                x_hi(0, 0)
                b0_hi(range(8, NBK))
                x_hi(1, 1)
                se.wait_ge(s_btab, 16)
            else:
                split_gu(0, 1, True)
            expert = [None]

            def body(it, last, now_shared, next_shared):
                for s in range(spi):
                    t, p = it * spi + s, s % 2
                    if layer == 2 and s % spb == 0:
                        expert[0] = se.value_load(eblk[0:1, ds(it * 2 + s // spb, 1)],
                                                  min_val=0, max_val=NE - 1)
                    se.wait_ge(s_gate, t + 1)
                    if layer == 1:
                        se.activation(gel[:, p, :], ps_gate[p][:, :], ACT.Gelu_apprx_tanh).then_inc(s_gel, 1)
                    else:
                        for c in range(2):
                            m = se.activation(gel[:, p, c * BT:(c + 1) * BT], ps_gate[p][:, c * BT:(c + 1) * BT],
                                              ACT.Silu, bias=btab[:, ds(expert[0] * 4 + (s % spb) * 2 + c, 1)])
                        m.then_inc(s_gel, 1)
                        u = s // spb
                        if s % spb == 0 and not (last and u == 1) and not (isinstance(it, int) and it + u == 0):
                            x_hi(2 * it + u + 1, 1 - u)
                    if not (last and s + 2 >= spi):
                        split_gu(it + (s + 2) // spi, (s + 2) % spi,
                                 now_shared if s + 2 < spi else next_shared)
                    se.wait_ge(s_act, t + 1)
                    wait(se, s_dn, t - 1)
                    se.activation(ahl[:, p, 0, :], act1[:, :], ACT.Copy).then_inc(s_ahi, 1)
                    if not (last and s + 1 >= spi):
                        split_dn(it + (s + 1) // spi, (s + 1) % spi)

            body(0, False, bool(n_sh), bool(n_sh))
            if n_sh:
                with se.Fori(1, n_sh - 1) as i:
                    body(i, False, True, True)
                body(n_sh - 1, False, True, False)
            with se.Fori(max(n_sh, 1), n_it - 1) as i:
                body(i, False, False, False)
            body(n_it - 1, True, False, False)
            if layer == 1:
                se.wait_ge(s_up, n_it * spi)
                for step, o, hi, _ in next_split:
                    se.wait_ge(s_raws[2][step], 16)
                    se.wait_ge(s_dn, n_it * spi - 1)
                    se.activation(whl[:, step, 0, o], raw[:, step, o], ACT.Copy).then_inc(ahead[hi], 1)

        @block.vector
        def _(dve):
            def split_gu(it, s):
                t, p = it * spi + s, s % 2
                dve.wait_ge(s_whi, t + 1)
                nc.vector.tensor_tensor(whl[:, p, 1, 0:GU], raw[:, s % RAWS, 0:GU],
                                        whl[:, p, 0, 0:GU].bitcast(F32), ALU.subtract).then_inc(s_wlo, 1)

            def split_dn(it, s):
                t, p = it * spi + s, s % 2
                dve.wait_ge(s_dhi, t + 1)
                nc.vector.tensor_tensor(whl[:, p, 1, GU:], raw[:, s % RAWS, GU:],
                                        whl[:, p, 0, GU:].bitcast(F32), ALU.subtract).then_inc(s_dlo, 1)

            def output(it, u, is_shared):
                b = it * 2 + u
                if layer == 2:
                    e = dve.value_load(eblk[0:1, ds(b, 1)], min_val=0, max_val=NE - 1)
                dve.wait_ge(s_dn, spb * (b + 1))
                src = ps_out[u][:, :].rearrange("p (k b t) -> p b k t", k=KD, b=BLK)
                if is_shared:
                    a = acc[:, ds(b * BLK, BLK), :, :]
                    nc.vector.tensor_tensor(a, a, src, ALU.add).then_inc(s_y, 1)
                    return
                slot0 = (b - 2 * n_sh) * BLK
                wait(dve, s_add, slot0)
                ys = y[:, :].rearrange("p (b k t) -> p b k t", b=BLK, k=KD)
                w = wslot[:, ds(slot0, BLK)].unsqueeze(2).broadcast_to([P, BLK, TOK])
                for k in range(KD):
                    if layer == 1:
                        m = nc.vector.tensor_tensor(ys[:, :, k, :], src[:, :, k, :], w, ALU.mult)
                    else:
                        m = nc.vector.scalar_tensor_tensor(ys[:, :, k, :], src[:, :, k, :],
                                                           btab[:, ds(NE * 8 + e * KD + k, 1)], w,
                                                           ALU.add, ALU.mult)
                m.then_inc(s_y, 1)

            def b0_lo(banks_m):
                for m in banks_m:
                    dve.wait_ge(s_b0hi, m + 1)
                    nc.vector.tensor_tensor(mixed(mem, 0, m, 1), built(banks[m % 4]),
                                            mixed(mem, 0, m, 0).bitcast(F32), ALU.subtract).then_inc(s_b0lo, 1)

            if layer == 2:
                b0_lo(range(NBK))
                dve.wait_ge(s_btab, 16)
            else:
                split_gu(0, 1)
            expert = [None]

            def body(it, last, prev_shared, now_shared):
                for s in range(spi):
                    t, p = it * spi + s, s % 2
                    if layer == 2 and s % spb == 0:
                        expert[0] = dve.value_load(eblk[0:1, ds(it * 2 + s // spb, 1)],
                                                   min_val=0, max_val=NE - 1)
                    dve.wait_ge(s_gel, t + 1)
                    dve.wait_ge(s_up, t + 1)
                    wait(dve, s_alo, t)
                    if layer == 1:
                        nc.vector.tensor_tensor(act1[:, :], ps_up[p][:, :], gel[:, p, :],
                                                ALU.mult).then_inc(s_act, 1)
                    else:
                        for c in range(2):
                            bias = btab[:, ds(expert[0] * 4 + NE * 4 + (s % spb) * 2 + c, 1)]
                            m = nc.vector.scalar_tensor_tensor(
                                act1[:, c * BT:(c + 1) * BT], ps_up[p][:, c * BT:(c + 1) * BT], bias,
                                gel[:, p, c * BT:(c + 1) * BT], ALU.add, ALU.mult)
                        m.then_inc(s_act, 1)
                    if not (last and s + 2 >= spi):
                        split_gu(it + (s + 2) // spi, (s + 2) % spi)
                    dve.wait_ge(s_ahi, t + 1)
                    nc.vector.tensor_tensor(ahl[:, p, 1, :], act1[:, :], ahl[:, p, 0, :].bitcast(F32),
                                            ALU.subtract).then_inc(s_alo, 1)
                    if not (last and s + 1 >= spi):
                        split_dn(it + (s + 1) // spi, (s + 1) % spi)
                    if s == spb:
                        output(it, 0, now_shared)
                    elif s == 0 and not (isinstance(it, int) and it == 0):
                        output(it - 1, 1, prev_shared)

            def next_lo(step, o, hi, lo, n):
                dve.wait_ge(ahead[hi], n)
                nc.vector.tensor_tensor(whl[:, step, 1, o], raw[:, step, o], whl[:, step, 0, o].bitcast(F32),
                                        ALU.subtract).then_inc(ahead[lo], 1)

            loop(dve, body)
            if layer == 1:
                next_lo(*next_split[0], 1)
            output(n_it - 1, 1, False)
            if layer == 1:
                next_lo(*next_split[1], 1)
                next_lo(*next_split[2], 2)


def layer3(nc, sem, mem, banks, s_b, bias3, out_tok):
    xg, acc, gel, bias3_b = (mem[k] for k in ("xg", "acc", "gel", "bias3_b"))
    ps_b, ps_o = banks[0:4], banks[4:8]

    s_xhi = sem("s_xhi_3")
    s_xlo0 = sem("s_xlo0_3")
    s_xlo = sem("s_xlo_3")
    s_bhi = sem("s_bhi")
    s_blo = sem("s_blo")
    s_p = sem("s_p")
    s_bias3 = sem("s_bias3")
    s_o = sem("s_o")
    s_out = [sem(f"s_out_{u}") for u in range(2)]
    s_out_last = sem("s_out_last")
    before_last = (NG - 1) * GB // 2

    def pair_of(g, p):
        if g + 1 == NG:
            ms = ()
        elif p == 0:
            ms = range(4)
        else:
            ms = range(2 * p + 2, min(2 * p + 4, NBK))
        return 8 * g + p, 4 * g + p // 2, ms

    def tokens(ap):
        return ap.rearrange("p k (b t) -> p k b t", b=BLK)

    def tile_lo(eng, tile, u, done):
        eng.wait_ge(s_xhi, tile + 1)
        eng.tensor_tensor(tokens(xg[:, u, KD:, :]), acc[:, ds(tile * BLK, BLK), :, :]
                          .rearrange("p b k t -> p k b t"),
                          tokens(xg[:, u, 0:KD, :].bitcast(F32)), ALU.subtract).then_inc(done, 1)

    def staged(pair):
        if isinstance(pair, int) and pair >= before_last:
            at = (pair - before_last) * 2 * CH
            ap = mem["parts"][0:TOK, at:at + 2 * CH].bitcast(F32)
        else:
            ap = gel[0:TOK, pair % 2, :]
        return ap.rearrange("p (b o) -> p b o", b=2)

    with nc.Block() as block:
        @block.tensor
        def _(pe):
            mm = nc.tensor.matmul

            for g in range(NG):
                for p in range(GB // 2):
                    pair, tile, ms = pair_of(g, p)
                    q, u = p % 4, tile % 2
                    if p == 0:
                        if g > 0:
                            for m in ms:
                                pe.wait_ge(s_blo, g * NBK + m - 3)
                                build_columns(mm, mem, g + 1, m, ps_b[m], range(PB)).then_inc(s_b, 1)
                        ms = ()
                        wait(pe, s_blo, NBK * g)
                    if p % 2 == 0:
                        pe.wait_ge(s_xlo if tile else s_xlo0, max(tile, 1))
                    wait(pe, s_o, pair - 3)
                    for b in range(2):
                        at = ((q % 2) * 2 + b) * TOK
                        w = [wbot(mem, g)[:, 2 * p + b, h, :] for h in range(2)]
                        if ms:
                            pe.wait_ge(s_blo, g * NBK + ms[b] - 3)
                        for k in range(KD):
                            m = split3(mm, ps_o[q][0:TOK, b * D:(b + 1) * D],
                                       xg[:, u, k, at:at + TOK], xg[:, u, KD + k, at:at + TOK],
                                       w[0][:, k * D:(k + 1) * D], w[1][:, k * D:(k + 1) * D],
                                       start=k == 0, stop=k == KD - 1)
                            if b == 1 and k == KD - 1:
                                m.then_inc(s_p, 1)
                            if ms:
                                c = build_columns(mm, mem, g + 1, ms[b], ps_b[ms[b] % 4],
                                                  range(k * PB // KD, (k + 1) * PB // KD))
                        if ms:
                            c.then_inc(s_b, 1)

        @block.scalar
        def _(se):
            def tile_hi(tile, u):
                wait(se, s_p, 2 * tile - 2)
                se.activation(tokens(xg[:, u, 0:KD, :]), acc[:, ds(tile * BLK, BLK), :, :]
                              .rearrange("p b k t -> p k b t"), ACT.Copy).then_inc(s_xhi, 1)

            def hi(g, m, e):
                se.wait_ge(s_b, (g - 1) * NBK + m + 1)
                se.activation(mixed(mem, g, m, 0), built(ps_b[e]), ACT.Copy).then_inc(s_bhi, 1)

            tile_hi(0, 0)

            for g in range(NG):
                for p in range(GB // 2):
                    _, tile, ms = pair_of(g, p)
                    if p == 0:
                        wait(se, s_p, 8 * g)
                    for m in ms:
                        hi(g + 1, m, m % 4)
                    if p % 2 == 0 and tile + 1 < NB // BLK:
                        tile_hi(tile + 1, (tile + 1) % 2)

        @block.gpsimd
        def _(pool):
            tile_lo(pool, 1, 1, s_xlo)
            with pool.Fori(1, NB // BLK // 2) as i:
                for u in range(2):
                    tile_lo(pool, 2 * i + u, u, s_xlo)

        @block.vector
        def _(dve):
            def lo(g, m, e):
                dve.wait_ge(s_bhi, (g - 1) * NBK + m + 1)
                nc.vector.tensor_tensor(mixed(mem, g, m, 1), built(ps_b[e]), mixed(mem, g, m, 0).bitcast(F32),
                                        ALU.subtract).then_inc(s_blo, 1)

            tile_lo(nc.vector, 0, 0, s_xlo0)
            for g in range(NG):
                for p in range(GB // 2):
                    pair, _, ms = pair_of(g, p)
                    for m in ms:
                        lo(g + 1, m, m % 4)
                    if pair == 0:
                        dve.wait_ge(s_bias3, 16)
                    dve.wait_ge(s_p, pair + 1)
                    if g < NG - 1:
                        wait(dve, s_out[p % 2], 16 * (pair // 2))
                    nc.vector.tensor_tensor(
                        staged(pair),
                        ps_o[p % 4][0:TOK, :].rearrange("p (b o) -> p b o", b=2),
                        bias3_b[0:TOK, :].unsqueeze(1).broadcast_to([TOK, 2, D]), ALU.add).then_inc(s_o, 1)

        @block.sync
        def _(sp):
            sp.dma_start(bias3_b[:, :], bias3).then_inc(s_bias3, 16)

            def store(pair, src, done):
                sp.wait_ge(s_o, pair + 1)
                sp.dma_start(out_tok[ds(pair * 2, 2), :, :].rearrange("b t o -> t b o"), src).then_inc(done, 16)

            with sp.Fori(0, before_last // 2) as i:
                for u in range(2):
                    store(2 * i + u, staged(u), s_out[u])
            for pair in range(before_last, NB // 2):
                store(pair, staged(pair), s_out_last)
            for u in range(2):
                sp.wait_ge(s_out[u], 16 * (before_last // 2))
            sp.wait_ge(s_out_last, 16 * (NB // 2 - before_last))


def laid_out(i):
    def steps(first, second, down):
        n = down.shape[-2] // STEPH
        cols = [w.reshape(-1, KD, P, n, STEPH).transpose(0, 3, 2, 1, 4).reshape(-1, n, P, CH)
                for w in (first, second)]
        cols.append(down.reshape(-1, n, 2, P, D).transpose(0, 1, 3, 2, 4).reshape(-1, n, P, CH))
        return np.concatenate(cols, axis=3)

    def by_feature(a, chunks):
        return np.moveaxis(a.reshape(a.shape[:-1] + (chunks, P)), -1, 0).reshape(P, -1)

    w_base_t = i["L0_cond_W_base"].T.reshape(KD, P, D).transpose(1, 0, 2).reshape(P, CH)
    as_t = i["L0_cond_As"].reshape(P, KD, P).transpose(2, 1, 0).reshape(P, D)
    bs_t = i["L0_cond_Bs"].transpose(0, 2, 1).reshape(P, D)
    cond = i["cond_8"]

    def by_slice(w):
        w = w.reshape(-1, D // SL, SL, KD, P).transpose(2, 0, 3, 1, 4)
        w = np.broadcast_to(w, (SL, NE) + w.shape[2:]).reshape(ROWP, QUARTERS, -1)
        return w.transpose(1, 0, 2).reshape(P, -1)

    row = np.arange(P)
    band = np.concatenate([row[:, None] + BAND == np.arange(BAND + P),
                           row[:, None] == np.repeat(np.arange(SL), GB)], axis=1)
    band[SL:] = False

    def tr(a):
        return a.transpose(0, 2, 1)

    return {
        "x": i["x"].reshape(NB, TOK, KD, P).transpose(3, 0, 2, 1),
        "cond": cond,
        "w0": np.concatenate([w_base_t, as_t, bs_t], axis=1),
        "wexp": np.repeat(cond.T, R_LORA, axis=0),
        "yrep": np.tile(cond.T, (P // NE, 1)),
        "delta": (row[:, None] // NE % SL == np.arange(SL)).astype(np.float32),
        "band": band.astype(np.float32),
        "w1": np.concatenate([
            steps(i["L1_cond_skill_gate"], i["L1_cond_skill_up"], i["L1_cond_skill_down"]),
            steps(i["L1_cond_shared_gate"], i["L1_cond_shared_up"], i["L1_cond_shared_down"])]),
        "w2": steps(tr(i["L2_cond_W_up"]), tr(i["L2_cond_W_gate"]), tr(i["L2_cond_W_down"])),
        "btab": np.concatenate([by_feature(i["L2_cond_b_up"], 4), by_feature(i["L2_cond_b_gate"], 4),
                                by_feature(i["L2_cond_b_down"], KD)], axis=1),
        "bias0": by_feature(i["L0_cond_b_base"], KD),
        "weight3": by_slice(i["L3_cond_weight"]),
        "mask3": by_slice(i["L3_cond_mask"][None]),
        "bias3": np.broadcast_to(i["L3_cond_bias"], (P, D)),
    }


def kernel(**inputs):
    import concourse.bacc as bacc
    from concourse.bass_utils import run_bass_kernel_spmd

    nc = bacc.Bacc("TRN2", target_bir_lowering=False, num_devices=1)
    arrays, d = {}, {}
    for name, a in laid_out({k: np.asarray(v) for k, v in inputs.items()}).items():
        a = np.ascontiguousarray(a)
        arrays[f"in_{name}"] = a
        d[name] = nc.dram_tensor(f"in_{name}", a.shape, mybir.dt.from_np(a.dtype), kind="ExternalInput").ap()
    out = nc.dram_tensor("out_0", (NB, TOK, D), F32, kind="ExternalOutput").ap()
    d["out"] = out
    build(nc, d)
    r = run_bass_kernel_spmd(nc, [arrays], core_ids=[0])
    return r.results[0]["out_0"]
```
